# Optimizing a Trainium2 kernel written in Bass

```python
import numpy as np
import jax
import jax.numpy as jnp

def _softmax(x, axis=-1):
    return jax.nn.softmax(x, axis=axis)

def _gelu(x):
    return jax.nn.gelu(x, approximate=True)

def _silu(x):
    return jax.nn.silu(x)

def _sigmoid(x):
    return jax.nn.sigmoid(x)

def _layernorm(x, axis=-1, eps=1e-05):
    m = jnp.mean(x, axis=axis, keepdims=True)
    v = jnp.var(x, axis=axis, keepdims=True)
    return (x - m) / jnp.sqrt(v + eps)

def _scatter_add(tgt, idx, src, axis=0):
    return tgt.at[idx].add(src)

def _segment_sum(src, seg, n):
    return jax.ops.segment_sum(src, seg, n)
kernel_name = 'mk_cond_resid_d2_seqx_r4_9cbcfe'

def setup_inputs(seed: int=0):
    np.random.seed(seed)
    _w = jnp.asarray

    def _rec_inputs():
        import jax
        import jax.numpy as jnp
        _rk = jax.random.key(seed)
        x = -0.0003929 + 0.9999 * jax.random.normal(jax.random.fold_in(_rk, 1), (32, 64, 1024), jnp.float32)
        _lenS = 64 - jax.random.randint(jax.random.fold_in(_rk, 7), (32,), 0, max(1, 64 // 4) + 1, jnp.int32)
        _lenS2 = 64 - jax.random.randint(jax.random.fold_in(_rk, 8), (32,), 0, max(1, 64 // 4) + 1, jnp.int32)
        itok_B_78_3631 = jax.random.randint(jax.random.fold_in(_rk, 11), (32,), 78, 908, jnp.int32)
        itok_B_0_23 = jax.random.randint(jax.random.fold_in(_rk, 12), (32,), 0, 24, jnp.int32)
        return (x, itok_B_78_3631, itok_B_0_23)
    x, itok_B_78_3631, itok_B_0_23 = _rec_inputs()

    def _L0_cond_setup():
        import math
        import jax, jax.numpy as jnp
        import numpy as np
        B, H, N, L = (16, 64, 64, 1024)
        DT_MIN, DT_MAX = (0.001, 0.1)

        def _get_kernel(log_dt, C, log_A_real, A_imag, length):
            dt = jnp.exp(log_dt)
            Cc = C[..., 0] + 1j * C[..., 1]
            A = -jnp.exp(log_A_real) + 1j * A_imag
            dtA = A * dt[:, None]
            Ct = Cc * (jnp.exp(dtA) - 1.0) / A
            P = dtA[:, :, None] * jnp.arange(length, dtype=jnp.float32)
            K = 2.0 * jnp.einsum('hn,hnl->hl', Ct, jnp.exp(P)).real
            return K
        key = jax.random.key(seed)
        ks = jax.random.split(key, 5)
        u = jax.random.normal(ks[0], (B, H, L), dtype=jnp.float32)
        log_dt = jax.random.uniform(ks[1], (H,), dtype=jnp.float32) * (math.log(DT_MAX) - math.log(DT_MIN)) + math.log(DT_MIN)
        C = jax.random.normal(ks[2], (H, N, 2), dtype=jnp.float32)
        log_A_real = jnp.log(0.5 * jnp.ones((H, N), dtype=jnp.float32))
        A_imag = math.pi * jnp.broadcast_to(jnp.arange(N, dtype=jnp.float32), (H, N))
        D = jax.random.normal(ks[3], (H,), dtype=jnp.float32)
        length = jax.random.randint(ks[4], (B,), 1, L + 1, dtype=jnp.int32)
        return {'u': u, 'log_dt': log_dt, 'C': C, 'log_A_real': log_A_real, 'A_imag': A_imag, 'D': D, 'length': length}
    _L0_cond_all = _L0_cond_setup()
    _L0_cond_in = {k: v for k, v in _L0_cond_all.items() if k in ('log_dt', 'C', 'log_A_real', 'A_imag', 'D')}
    del _L0_cond_all

    def _L1_cond_setup():
        import jax, jax.numpy as jnp
        import numpy as np
        R = 16
        ALPHA = 32
        SCALING = ALPHA / R
        SLOTS = 32
        IN_F = 1024
        OUT_F = 1024
        B, T = (8, 256)
        key = jax.random.key(seed)
        k1, k2, k3, k4, k5, k6 = jax.random.split(key, 6)
        x = jax.random.normal(k1, (B, T, IN_F), dtype=jnp.float32)
        adapter_mapping = jax.random.randint(k2, (B,), 0, SLOTS, dtype=jnp.int32)
        W = jax.random.normal(k3, (OUT_F, IN_F), dtype=jnp.float32) * 0.02
        b = jax.random.normal(k4, (OUT_F,), dtype=jnp.float32) * 0.02
        lora_As = jax.random.normal(k5, (SLOTS, IN_F, R), dtype=jnp.float32) * 0.02
        lora_Bs = jax.random.normal(k6, (SLOTS, R, OUT_F), dtype=jnp.float32) * 0.02
        return {'x': x, 'adapter_mapping': adapter_mapping, 'W': W, 'b': b, 'lora_As': lora_As, 'lora_Bs': lora_Bs}
    _L1_cond_all = _L1_cond_setup()
    _L1_cond_in = {k: v for k, v in _L1_cond_all.items() if k in ('W', 'b', 'lora_As', 'lora_Bs')}
    del _L1_cond_all
    return {'x': x, 'itok_B_78_3631': itok_B_78_3631, 'itok_B_0_23': itok_B_0_23, 'L0_cond_log_dt': _L0_cond_in['log_dt'], 'L0_cond_C': _L0_cond_in['C'], 'L0_cond_log_A_real': _L0_cond_in['log_A_real'], 'L0_cond_A_imag': _L0_cond_in['A_imag'], 'L0_cond_D': _L0_cond_in['D'], 'L1_cond_W': _L1_cond_in['W'], 'L1_cond_b': _L1_cond_in['b'], 'L1_cond_lora_As': _L1_cond_in['lora_As'], 'L1_cond_lora_Bs': _L1_cond_in['lora_Bs']}

def reference(x, itok_B_78_3631, itok_B_0_23, L0_cond_log_dt, L0_cond_C, L0_cond_log_A_real, L0_cond_A_imag, L0_cond_D, L1_cond_W, L1_cond_b, L1_cond_lora_As, L1_cond_lora_Bs):
    import jax
    import jax.numpy as jnp

    def _L0_cond_ref(u, log_dt, C, log_A_real, A_imag, D, length):
        import math
        import jax, jax.numpy as jnp
        import numpy as np
        B, H, N, L = (16, 64, 64, 1024)
        DT_MIN, DT_MAX = (0.001, 0.1)

        def _get_kernel(log_dt, C, log_A_real, A_imag, length):
            dt = jnp.exp(log_dt)
            Cc = C[..., 0] + 1j * C[..., 1]
            A = -jnp.exp(log_A_real) + 1j * A_imag
            dtA = A * dt[:, None]
            Ct = Cc * (jnp.exp(dtA) - 1.0) / A
            P = dtA[:, :, None] * jnp.arange(length, dtype=jnp.float32)
            K = 2.0 * jnp.einsum('hn,hnl->hl', Ct, jnp.exp(P)).real
            return K
        Bq, Hq, Lq = u.shape
        K = _get_kernel(log_dt, C, log_A_real, A_imag, Lq)
        n = 2 * Lq
        kf = jnp.fft.rfft(K, n=n)
        uf = jnp.fft.rfft(u, n=n)
        y = jnp.fft.irfft(uf * kf[None], n=n)[..., :Lq]
        y = y + u * D[:, None]
        mask = (jnp.arange(Lq)[None, :] < length[:, None]).astype(u.dtype)
        return y * mask[:, None, :]

    def _L1_cond_ref(x, adapter_mapping, W, b, lora_As, lora_Bs):
        import jax, jax.numpy as jnp
        import numpy as np
        R = 16
        ALPHA = 32
        SCALING = ALPHA / R
        SLOTS = 32
        IN_F = 1024
        OUT_F = 1024
        B, T = (8, 256)
        base_out = jnp.einsum('bti,oi->bto', x, W) + b
        A = lora_As[adapter_mapping]
        Bm = lora_Bs[adapter_mapping]
        lora_h = jnp.einsum('bti,bir->btr', x, A)
        lora_out = jnp.einsum('btr,bro->bto', lora_h, Bm)
        return base_out + lora_out * SCALING
    x = x + _L0_cond_ref(x, L0_cond_log_dt, L0_cond_C, L0_cond_log_A_real, L0_cond_A_imag, L0_cond_D, itok_B_78_3631)
    x = x + _L1_cond_ref(x, itok_B_0_23, L1_cond_W, L1_cond_b, L1_cond_lora_As, L1_cond_lora_Bs)
    return x

_drawn_inputs = setup_inputs


def setup_inputs(seed=0):
    import zlib

    import numpy as np

    out = dict(_drawn_inputs(seed))
    spreads = {'L0_cond_log_A_real': (-0.6931471824645996, 0.2)}
    factors = {'L1_cond_b': 5.485}
    for name, (base, spread) in spreads.items():
        noise = np.random.default_rng([zlib.crc32(name.encode()), seed]).standard_normal(out[name].shape)
        drawn = base * np.exp(spread * noise) if base else spread * noise
        out[name] = jnp.asarray(drawn.astype(out[name].dtype))
    for name, factor in factors.items():
        out[name] = (out[name] * factor).astype(out[name].dtype)
    return out
```

```python
from contextlib import ExitStack

import concourse.bass as bass
from concourse import mybir

ALU = mybir.AluOpType
ACT = mybir.ActivationFunctionType
AX_X = mybir.AxisListType.X
F32 = mybir.dt.float32
F32R = mybir.dt.float32r
I32 = mybir.dt.int32

P = 128
B, H, L = 32, 64, 1024
N = 64
Q = 128
ND = L // Q
G = 8
NG = H // G
R = 16
SLOTS = 32
NT = B // 2
PI = 3.141592653589793
TWO_PI = 6.2831850
ROUND = 12582912.0

NJ = Q + 1
MA, MB = 8, 16
C_J, C_EYE, C_REV, C_M2, C_OFF, C_OFFX, C_LPOS, C_EXP, C_BM, C_SEL, C_END = (
    0, 129, 257, 385, 449, 450, 451, 459, 483, 611, 613)


def constants():
    import numpy as np
    c = np.zeros((P, C_END), np.float32)
    p = np.arange(P)
    c[:, C_J:C_J + NJ] = np.arange(NJ)
    c[:, C_EYE:C_EYE + P] = np.eye(P)
    c[:, C_REV:C_REV + P] = np.eye(P)[::-1]
    c[:, C_M2:C_M2 + N] = (p[:, None] % N == np.arange(N)[None, :])
    c[:, C_OFF] = np.where(p < N, 0.25, 0.5)
    c[:, C_OFFX] = np.where(p < N, 0.0, 0.5)
    c[:, C_LPOS:C_LPOS + ND] = p[:, None] + Q * np.arange(ND)[None, :]
    c[:, C_EXP:C_EXP + MB] = 1 + np.arange(MB)
    c[:, C_EXP + MB:C_EXP + MB + MA] = MB * np.arange(MA)
    c[:2 * R, C_BM:C_BM + P] = 2.0 * (p[:2 * R, None] // R == np.arange(P)[None, :] // H)
    c[3 * 32, C_SEL] = 1.0
    c[3 * 32 + 1, C_SEL + 1] = 1.0
    return c


def conv_then_lora(nc, xT, par, dvec, lens, slots, wT, bias2, loraA, loraB, consts, out):
    kpad = nc.dram_tensor("kpad", [2, G, 2 * Q], F32, kind="Internal").ap()

    with ExitStack() as ctx:
        def sb(name, shape, dt=F32, stack=ctx):
            return stack.enter_context(nc.sbuf_tensor(name, shape, dt))

        def sem(name):
            return ctx.enter_context(nc.semaphore(name))

        x = sb("x", [P, H, ND * B])
        w_hi = sb("w_hi", [P, ND, L], F32R)
        w_lo = sb("w_lo", [P, ND, L], F32R)
        cst = sb("cst", [P, C_END])
        slot_ids = sb("slot_ids", [1, B], I32)
        credit = sb("credit", [1, 8])
        one = ExitStack()
        modes = sb("modes", [P, H, MB + MA], stack=one)
        mag = sb("mag", [P, G, Q], stack=one)
        turn = sb("turn", [P, G, NJ], stack=one)
        phase = sb("phase", [P, G, NJ], stack=one)
        w_raw = sb("w_raw", [P, L], stack=one)
        exps = [sb(f"exps{u}", [P, G, NJ], stack=one) for u in range(2)]
        exps_rev = sb("exps_rev", [P, G, Q], stack=one)
        vin = sb("vin", [P, G, P], stack=one)
        rot = sb("rot", [P, G, 2, N], stack=one)
        hank = sb("hank", [P, G, Q], stack=one)
        toep = [sb(f"toep{u}", [P, G, Q], stack=one) for u in range(2)]
        st = [sb(f"st{u}", [P, G, ND - 1, B], stack=one) for u in range(2)]
        sa = sb("sa", [P, G, B], stack=one)
        sx = sb("sx", [P, G, B], stack=one)
        ym = [sb(f"ym{u}", [P, 2, ND * B], stack=one) for u in range(2)]
        prm = exps[1][:].rearrange("p g j -> p (g j)")[:, 0:5 * H].rearrange("p (k h) -> p k h", k=5)
        freq = sb("freq", [P, H + G], stack=one)
        lam_own = sb("lam_own", [P, H], stack=one)
        lam_cross = sb("lam_cross", [P, H], stack=one)
        coef = sb("coef", [P, H, 2], stack=one)
        mask = sb("mask", [P, ND, B], stack=one)
        len_sb = sb("len_sb", [P, B], I32, stack=one)
        d_sb = sb("d_sb", [G, NG], stack=one)
        kcol = sb("kcol", [P, G], stack=one)
        krow = sb("krow", [G, Q], stack=one)
        zero = hank[0:2 * G, 0, :]
        one.close()
        two = ExitStack()
        a_raw = [sb(f"a_raw{u}", [P, 2, P], stack=two) for u in range(2)]
        b_raw = [sb(f"b_raw{u}", [2 * R, L], stack=two) for u in range(2)]
        a_hi = [sb(f"a_hi{u}", [P, ND, 2 * R], F32R, stack=two) for u in range(2)]
        a_lo = [sb(f"a_lo{u}", [P, ND, 2 * R], F32R, stack=two) for u in range(2)]
        xs_hi = [sb(f"xs_hi{u}", [P, ND, P], F32R, stack=two) for u in range(2)]
        xs_lo = [sb(f"xs_lo{u}", [P, ND, P], F32R, stack=two) for u in range(2)]
        KB = 3 * 32 + 2
        b_stk = [sb(f"b_stk{u}", [KB, L], F32R, stack=two) for u in range(2)]
        h_stk = [sb(f"h_stk{u}", [KB, P], F32R, stack=two) for u in range(2)]
        h_f32 = sb("h_f32", [2 * R, P], stack=two)
        bias = sb("bias", [KB, L], stack=two)
        bias_t = sb("bias_t", [KB, L], stack=two)
        res = [sb(f"res{u}", [P, L], stack=two) for u in range(2)]
        two.close()

        psU = ctx.enter_context(nc.psum_tensor("psU", [P, G, 256], F32))
        psY = ctx.enter_context(nc.psum_tensor("psY", [P, 2, 512], F32))
        psV = ctx.enter_context(nc.psum_tensor("psV", [P, 2, 512], F32))

        in_small = sem("in_small")
        in_x = [sem(f"in_x{u}") for u in range(2)]
        in_w = sem("in_w")
        zeros_made = sem("zeros_made")
        zeros_stored = sem("zeros_stored")
        k_stored = sem("k_stored")
        hankel_in = sem("hankel_in")
        flipped = sem("flipped")
        toep_ready = sem("toep_ready")
        dve_step = sem("dve_step")
        act_param = sem("act_param")
        freq_ready = sem("freq_ready")
        lam_args = sem("lam_args")
        turn_ready = sem("turn_ready")
        whole_ready = sem("whole_ready")
        frac_ready = sem("frac_ready")
        sin_ready = sem("sin_ready")
        modes_ready = sem("modes_ready")
        mag_ready = sem("mag_ready")
        coef_ready = sem("coef_ready")
        rot_ready = sem("rot_ready")
        exps_ready = sem("exps_ready")
        rev_ready = sem("rev_ready")
        v_made = sem("v_made")
        v_ready = sem("v_ready")
        u_ready = sem("u_ready")
        kcol_ready = sem("kcol_ready")
        k_turned = sem("k_turned")
        krow_ready = sem("krow_ready")
        scan_step = sem("scan_step")
        y_ready = sem("y_ready")
        masked = sem("masked")
        added = sem("added")
        w_eye = sem("w_eye")
        w_hi_ready = sem("w_hi_ready")
        w_lo_ready = sem("w_lo_ready")
        in_a = [sem(f"in_a{u}") for u in range(2)]
        in_b = [sem(f"in_b{u}") for u in range(2)]
        in_bias = sem("in_bias")
        xs_hi_ready = sem("xs_hi_ready")
        xs_lo_ready = sem("xs_lo_ready")
        a_hi_ready = sem("a_hi_ready")
        a_lo_ready = sem("a_lo_ready")
        b_hi_ready = sem("b_hi_ready")
        b_ready = sem("b_ready")
        h_ready = sem("h_ready")
        h_step = sem("h_step")
        out_ready = sem("out_ready")
        out_taken = sem("out_taken")
        out_stored = [sem(f"out_stored{u}") for u in range(2)]

        STEPS = 1 + 5 * (ND - 2)
        YQ = G // 2
        A_DRAM = loraA
        B_DRAM = loraB

        block = ctx.enter_context(nc.Block())

        @block.sync
        def _(sp):
            def load_x(g, u):
                sp.dma_start(x[:, bass.ds(g * G, G), :], xT[:, bass.ds(g * G, G), :]).then_inc(in_x[u], 16)

            def load_w(g):
                sp.dma_start(w_raw[:], wT[:, bass.ds(g, 1), :].rearrange("p c o -> p (c o)")).then_inc(in_w, 16)

            def hankel(q, u, first=False):
                sp.wait_ge(krow_ready, q * 2 + 2)
                sp.dma_start(kpad[u, :, Q:2 * Q], krow[:]).then_inc(k_stored, 16)
                sp.wait_ge(k_stored, q * 16 + 16)
                if not first:
                    sp.wait_ge(flipped, q * 2)
                src = bass.AP(tensor=kpad.tensor, offset=u * G * 2 * Q + 1, ap=[[1, P], [2 * Q, G], [1, Q]])
                sp.dma_start(hank[:], src).then_inc(hankel_in, 16)

            sp.dma_start(prm, par).then_inc(in_small, 16)
            sp.dma_start(cst[:], consts).then_inc(in_small, 16)
            sp.dma_start(len_sb[:], lens).then_inc(in_small, 16)
            sp.dma_start(d_sb[:], dvec).then_inc(in_small, 16)
            sp.dma_start(slot_ids[:], slots).then_inc(in_small, 16)
            load_x(0, 0)
            sp.wait_ge(zeros_made, 1)
            sp.dma_start(kpad[:, :, 0:Q].rearrange("u c q -> (u c) q"), zero).then_inc(zeros_stored, 16)
            load_w(0)
            load_x(1, 1)
            sp.wait_ge(zeros_stored, 16)
            hankel(0, 0, first=True)

            def group(g, u, i, more_x=True):
                if more_x:
                    sp.wait_ge(in_x[u], i * 16 + 16)
                    load_x(g + 2, u)
                hankel(g + 1, 1 - u)
                sp.wait_ge(w_lo_ready, g + 1)
                load_w(g + 1)

            with sp.Fori(0, 3) as i:
                for u in range(2):
                    group(i * 2 + u, u, i)
            group(6, 0, 3, more_x=False)

            def load_ab(t, u):
                for k in range(2):
                    s = sp.value_load(slot_ids[0:1, bass.ds(t * 2 + k, 1)], min_val=0, max_val=SLOTS - 1)
                    sp.dma_start(a_raw[u][:, k, :],
                                 A_DRAM[bass.ds(s, 1)].rearrange("s p f -> (s p) f")).then_inc(in_a[u], 16)
                    sp.dma_start(b_raw[u][R * k:R * k + R, :],
                                 B_DRAM[bass.ds(s, 1)].rearrange("s r f -> (s r) f")).then_inc(in_b[u], 16)

            sp.wait_ge(exps_ready, 2 * NG)
            load_ab(0, 0)
            load_ab(1, 1)
            sp.wait_ge(added, 2 + NG * YQ)
            sp.dma_start(bias[3 * 32:KB, :], bias2).then_inc(in_bias, 16)

            def tile(t, u, last=False):
                if not last:
                    sp.wait_ge(a_lo_ready, t + 1)
                    sp.wait_ge(b_ready, t + 1)
                    load_ab(t + 2, u)
                sp.wait_ge(out_taken, t * 2 + 4 + 2)
                sp.dma_start(out[bass.ds(t * P, P), :], res[u][:]).then_inc(out_stored[u], 16)

            with sp.Fori(0, NT // 2 - 1) as i:
                for u in range(2):
                    tile(i * 2 + u, u)
            for u in range(2):
                tile(NT - 2 + u, u, last=True)
            for u in range(2):
                sp.wait_ge(out_stored[u], 16 * (NT // 2 + 1))

        @block.tensor
        def _(pe):
            def make_v(q):
                early = isinstance(q, int) and q < 2
                pe.wait_ge(rot_ready, q + 1)
                pe.wait_ge(rev_ready, q + 1)
                for half in range(2):
                    if not early:
                        pe.wait_ge(toep_ready, q * 2 - 4 + half + 1)
                    elif q == 1:
                        pe.wait_ge(v_ready, half + 1)
                    if half == 0 and not (early and q == 0):
                        pe.wait_ge(krow_ready, q * 2)
                    for k in range(4):
                        c = 4 * half + k
                        mm = pe.matmul(psV[:, half, k * P:(k + 1) * P], exps_rev[:, c, :],
                                       rot[:, c, :, :].rearrange("p a n -> p (a n)"), start=True, stop=True)
                    mm.then_inc(v_made, 1)

            def inject(q, u, i, first=False):
                pe.wait_ge(v_ready, q * 2 + 2)
                pe.wait_ge(in_x[u], i * 16 + 16)
                if not first:
                    pe.wait_ge(scan_step, q * STEPS)
                for c in range(G):
                    mm = pe.matmul(psU[:, c, 0:(ND - 1) * B], vin[:, c, :],
                                   x[:, bass.ds(q * G + c, 1), 0:(ND - 1) * B].rearrange("p a f -> p (a f)"),
                                   start=True, stop=True)
                mm.then_inc(u_ready, 1)
                pe.wait_ge(kcol_ready, q + 1)
                if not first:
                    pe.wait_ge(toep_ready, q * 2 - 1)
                pe.matmul(psV[0:G, 0, 0:Q], kcol[:], cst[:, C_REV:C_REV + Q],
                          start=True, stop=True).then_inc(k_turned, 1)

            def flip(q, last=False):
                pe.wait_ge(hankel_in, q * 16 + 16)
                for half in range(2):
                    if not last:
                        pe.wait_ge(v_ready, q * 2 + 2 + half + 1)
                    if last and half == 0:
                        pe.wait_ge(krow_ready, 2 * NG)
                    pe.matmul(psV[:, half, :], cst[:, C_REV:C_REV + Q],
                              hank[:, 4 * half:4 * half + 4, :].rearrange("p c j -> p (c j)"),
                              start=True, stop=True).then_inc(flipped, 1)

            def outputs(g, u):
                pe.wait_ge(toep_ready, g * 2 + 2)
                pe.wait_ge(scan_step, g * STEPS + STEPS)
                for r in range(YQ):
                    pe.wait_ge(masked, g * YQ + r + 1)
                    for k in range(2):
                        c = 2 * r + k
                        pe.matmul(psY[:, r % 2, k * 256:(k + 1) * 256], toep[u][:, c, :],
                                  x[:, bass.ds(g * G + c, 1), :].rearrange("p a f -> p (a f)"),
                                  start=True, stop=False)
                        mm = pe.matmul(psY[:, r % 2, k * 256 + B:(k + 1) * 256], exps[u][:, c, 1:NJ],
                                       st[u][:, c, :, :].rearrange("p d b -> p (d b)"), start=False, stop=True)
                    mm.then_inc(y_ready, 1)

            pe.wait_ge(in_small, 80)
            make_v(0)
            inject(0, 0, 0, first=True)
            make_v(1)
            flip(0)
            with pe.Fori(0, 3) as i:
                for u in range(2):
                    g = i * 2 + u
                    inject(g + 1, 1 - u, i + u)
                    outputs(g, u)
                    make_v(g + 2)
                    flip(g + 1)
            inject(7, 1, 3)
            outputs(6, 0)
            flip(7, last=True)
            outputs(7, 1)

            def tile(t, u):
                acc = psU[:, 4 * u:4 * u + 4, :].rearrange("p a f -> p (a f)")
                hp = psY[0:2 * R, u, 0:P]
                pe.wait_ge(xs_lo_ready, t + 1)
                pe.wait_ge(a_lo_ready, t + 1)
                n = 0
                for c in range(ND):
                    for a, v in ((a_hi, xs_hi), (a_lo, xs_hi), (a_hi, xs_lo)):
                        mm = pe.matmul(hp, a[u][:, c, :], v[u][:, c, :],
                                       start=(n == 0), stop=(n == 3 * ND - 1))
                        n += 1
                mm.then_inc(h_ready, 1)
                pe.wait_ge(w_lo_ready, NG)
                pe.wait_ge(out_taken, t * 2 + 2)
                for half in range(2):
                    cols = slice(512 * half, 512 * half + 512)
                    for c in range(ND):
                        for v, w in ((xs_hi, w_hi), (xs_hi, w_lo), (xs_lo, w_hi)):
                            pe.matmul(acc[:, cols], v[u][:, c, :], w[:, c, cols],
                                      start=(c == 0 and w is w_hi and v is xs_hi), stop=False)
                    if half == 0:
                        pe.wait_ge(h_step, t * 4 + 4)
                        pe.wait_ge(b_ready, t + 1)
                    pe.matmul(acc[:, cols], h_stk[u][:, :], b_stk[u][:, cols],
                              start=False, stop=True).then_inc(out_ready, 1)

            with pe.Fori(0, NT // 2) as i:
                for u in range(2):
                    tile(i * 2 + u, u)

        @block.scalar
        def _(act):
            def turns(q):
                if not (isinstance(q, int) and q == 0):
                    act.wait_ge(frac_ready, q)
                for c in range(G):
                    a = act.activation(turn[:, c, :], cst[:, C_J:C_J + NJ], ACT.Identity,
                                       bias=cst[:, C_OFF:C_OFF + 1], scale=freq[:, bass.ds(q * G + c, 1)])
                a.then_inc(turn_ready, 1)

            def sines(q):
                act.wait_ge(frac_ready, q + 1)
                act.activation(phase[:], phase[:], ACT.Sin, scale=TWO_PI).then_inc(sin_ready, 1)

            def reverse(q):
                act.wait_ge(exps_ready, q * 2 + 2)
                if not (isinstance(q, int) and q == 0):
                    act.wait_ge(v_made, q * 2)
                act.activation(exps_rev[:], exps_of(q)[:, :, Q - 1::-1], ACT.Copy).then_inc(rev_ready, 1)

            def exps_of(q):
                return exps[par_of[0]]

            par_of = [0]

            def copy_v(q):
                for half in range(2):
                    act.wait_ge(v_made, q * 2 + half + 1)
                    if half == 0 and not (isinstance(q, int) and q == 0):
                        act.wait_ge(u_ready, q)
                        act.wait_ge(kcol_ready, q)
                    act.activation(vin[:, 4 * half:4 * half + 4, :].rearrange("p c s -> p (c s)"),
                                   psV[:, half, :], ACT.Copy).then_inc(v_ready, 1)

            def copy_toep(q, u):
                for half in range(2):
                    act.wait_ge(flipped, q * 2 + half + 1)
                    if half == 0 and not (isinstance(q, int) and q < 2):
                        act.wait_ge(masked, q * YQ - YQ + 2)
                    act.activation(toep[u][:, 4 * half:4 * half + 4, :].rearrange("p c j -> p (c j)"),
                                   psV[:, half, :], ACT.Copy).then_inc(toep_ready, 1)

            def split_w(g):
                act.wait_ge(w_eye, g + 1)
                act.activation(w_hi[:, bass.ds(g, 1), :].rearrange("p c o -> p (c o)"), w_raw[:],
                               ACT.Copy).then_inc(w_hi_ready, 1)

            tmp = st[1][:].rearrange("p g d b -> p (g d b)")
            act.wait_ge(in_small, 80)
            act.activation(tmp[:, 0:H], prm[:, 0, :], ACT.Exp).then_inc(act_param, 1)
            act.activation(tmp[:, H:2 * H], prm[:, 1, :], ACT.Exp).then_inc(act_param, 1)
            act.wait_ge(lam_args, 1)
            act.activation(tmp[:, 4 * H:5 * H], tmp[:, 2 * H:3 * H], ACT.Tanh, scale=0.5).then_inc(act_param, 1)
            act.activation(tmp[:, 5 * H:6 * H], tmp[:, 2 * H:3 * H], ACT.Exp, scale=float(Q)).then_inc(act_param, 1)
            act.wait_ge(freq_ready, 1)
            turns(0)
            act.wait_ge(lam_args, 2)
            act.activation(modes[:], modes[:], ACT.Exp).then_inc(modes_ready, 1)
            sines(0)
            act.wait_ge(lam_args, 3)
            act.activation(tmp[:, 8 * H:12 * H], tmp[:, 8 * H:12 * H], ACT.Sin, scale=TWO_PI).then_inc(act_param, 1)
            turns(1)
            par_of[0] = 0
            reverse(0)
            copy_v(0)
            sines(1)
            turns(2)
            par_of[0] = 1
            reverse(1)
            copy_v(1)
            copy_toep(0, 0)

            with act.Fori(0, 3) as i:
                for u in range(2):
                    g = i * 2 + u
                    sines(g + 2)
                    turns(g + 3)
                    split_w(g)
                    par_of[0] = u
                    reverse(g + 2)
                    copy_v(g + 2)
                    copy_toep(g + 1, 1 - u)
            copy_toep(7, 1)
            split_w(6)
            split_w(7)

            def split_x(t, u):
                act.wait_ge(out_ready, t * 2 + 2)
                act.activation(xs_hi[u][:].rearrange("p d (b h) -> p d b h", b=2),
                               x[:].rearrange("p h (d b) -> p d b h", b=B)[:, :, bass.ds(t * 2, 2), :],
                               ACT.Copy).then_inc(xs_hi_ready, 1)

            def split_a(t, u, i):
                act.wait_ge(in_a[u], i * 32 + 32)
                act.activation(a_hi[u][:].rearrange("p c (k r) -> p c k r", k=2),
                               a_raw[u][:].rearrange("p k (c r) -> p c k r", r=R), ACT.Copy).then_inc(a_hi_ready, 1)

            def take(t, u, i):
                for half in range(2):
                    act.wait_ge(out_ready, t * 2 + 4 + half + 1)
                    if half == 0:
                        act.wait_ge(out_stored[u], i * 16 + 16)
                    act.activation(res[u][:, 512 * half:512 * half + 512],
                                   psU[:, 4 * u + 2 * half:4 * u + 2 * half + 2, :].rearrange("p a f -> p (a f)"),
                                   ACT.Copy).then_inc(out_taken, 1)

            act.wait_ge(added, 2 + NG * YQ)
            split_x(0, 0)
            split_a(0, 0, 0)
            with act.Fori(0, NT // 2 - 1) as i:
                for u in range(2):
                    t = i * 2 + u
                    split_x(t + 1, 1 - u)
                    split_a(t + 1, 1 - u, i + u)
                    take(t, u, i)
            split_x(NT - 1, 1)
            split_a(NT - 1, 1, NT // 2 - 1)
            take(NT - 2, 0, NT // 2 - 1)
            take(NT - 1, 1, NT // 2 - 1)

        @block.vector
        def _(dve):
            count = [0]

            def step(ins):
                count[0] += 1
                ins.then_inc(dve_step, 1)
                dve.wait_ge(dve_step, count[0])

            tmp = st[1][:].rearrange("p g d b -> p (g d b)")

            def col(k, n=1):
                return tmp[:, k * H:(k + n) * H]

            dt, ea, decay, theta, tanh, eq = (col(k) for k in range(6))
            are, t0, args = col(6), col(7), col(8, 4)
            cr, ci, aim = prm[:, 3, :], prm[:, 4, :], prm[:, 2, :]

            def whole(q):
                dve.wait_ge(turn_ready, q + 1)
                dve.tensor_scalar(phase[:], turn[:], ROUND, -ROUND, ALU.add, ALU.add).then_inc(whole_ready, 1)

            def powers(q, u, first=False):
                dve.wait_ge(sin_ready, q + 1)
                dve.wait_ge(mag_ready, q + 1)
                if not first:
                    dve.wait_ge(y_ready, q * YQ - YQ)
                dve.tensor_tensor(exps[u][:, :, 1:NJ], phase[:, :, 1:NJ], mag[:], ALU.mult).then_inc(exps_ready, 1)
                dve.tensor_copy(exps[u][:, :, 0:1], phase[:, :, 0:1]).then_inc(exps_ready, 1)

            def sum_k(q, first=False):
                dve.wait_ge(v_ready, q * 2 + 2)
                if not first:
                    dve.wait_ge(k_turned, q)
                dve.tensor_reduce(kcol[:], vin[:, :, 0:N], AX_X, ALU.add).then_inc(kcol_ready, 1)

            def k_rows(q, first=False):
                dve.wait_ge(k_turned, q + 1)
                if not first:
                    dve.wait_ge(k_stored, q * 16)
                dve.tensor_copy(krow[:, 1:Q], psV[0:G, 0, 1:Q]).then_inc(krow_ready, 1)
                dve.tensor_tensor(krow[:, 0:1], psV[0:G, 0, 0:1], d_sb[:, bass.ds(q, 1)],
                                  ALU.add).then_inc(krow_ready, 1)

            def mask_y(g, r):
                dve.wait_ge(y_ready, g * YQ + r + 1)
                dve.wait_ge(added, g * YQ + r + 1)
                m = mask[:].rearrange("p d b -> p (d b)").unsqueeze(1).to_broadcast([P, 2, ND * B])
                dve.tensor_tensor(ym[r % 2][:], psY[:, r % 2, :].rearrange("p (a f) -> p a f", a=2), m,
                                  ALU.mult).then_inc(masked, 1)

            def scan(q, u, between):
                base = q * STEPS
                dve.wait_ge(u_ready, q + 1)
                s = st[u]
                own = lam_own[:, bass.ds(q * G, G)].unsqueeze(2).to_broadcast([P, G, B])
                cross = lam_cross[:, bass.ds(q * G, G)].unsqueeze(2).to_broadcast([P, G, B])
                dve.tensor_copy(s[:, :, 0, :], psU[:, :, 0:B]).then_inc(scan_step, 1)
                between(0)
                for d in range(1, ND - 1):
                    done = base + (1 + 5 * (d - 1))
                    dve.wait_ge(scan_step, done)
                    dve.tensor_tensor(sa[:], s[:, :, d - 1, :], own, ALU.mult).then_inc(scan_step, 1)
                    dve.tensor_tensor(sx[0:N], s[N:P, :, d - 1, :], cross[N:P], ALU.mult).then_inc(scan_step, 1)
                    dve.tensor_tensor(sx[N:P], s[0:N, :, d - 1, :], cross[0:N], ALU.mult).then_inc(scan_step, 1)
                    dve.wait_ge(scan_step, done + 1)
                    dve.tensor_tensor(sa[:], sa[:], psU[:, :, d * B:(d + 1) * B], ALU.add).then_inc(scan_step, 1)
                    dve.wait_ge(scan_step, done + 4)
                    dve.tensor_tensor(s[:, :, d, :], sa[:], sx[:], ALU.add).then_inc(scan_step, 1)
                    between(d)

            dve.memset(zero, 0.0).then_inc(zeros_made, 1)
            dve.wait_ge(in_small, 80)
            dve.wait_ge(act_param, 2)
            dve.tensor_tensor(theta, aim, dt, ALU.mult).then_inc(dve_step, 1)
            count[0] += 1
            step(dve.tensor_scalar(are, ea, -1.0, None, ALU.mult))
            dve.tensor_tensor(decay, are, dt, ALU.mult).then_inc(lam_args, 1)
            step(dve.memset(freq[:, H:H + G], 0.0))
            dve.tensor_scalar(freq[:, 0:H], theta, 1.0 / (2 * PI), None, ALU.mult).then_inc(freq_ready, 1)
            dve.wait_ge(lam_args, 1)
            jm = cst[:, C_EXP:C_EXP + MA + MB].unsqueeze(1).to_broadcast([P, H, MA + MB])
            dve.tensor_tensor(modes[:], decay.unsqueeze(2).to_broadcast([P, H, MA + MB]), jm,
                              ALU.mult).then_inc(lam_args, 1)
            whole(0)
            dve.wait_ge(freq_ready, 1)
            f = freq[:, 0:H]
            dve.tensor_scalar(args[:, 0:H], f, float(Q), 0.25, ALU.mult, ALU.add).then_inc(dve_step, 1)
            dve.tensor_scalar(args[:, H:2 * H], f, float(Q), cst[:, C_OFFX:C_OFFX + 1], ALU.mult,
                              ALU.add).then_inc(dve_step, 1)
            count[0] += 2
            step(dve.tensor_copy(args[:, 2 * H:3 * H], f))
            wh = col(12, 3)
            step(dve.tensor_scalar(wh, args[:, 0:3 * H], ROUND, -ROUND, ALU.add, ALU.add))
            step(dve.tensor_tensor(args[:, 0:3 * H], args[:, 0:3 * H], wh, ALU.subtract))
            dve.tensor_scalar(args[:, 3 * H:4 * H], args[:, 2 * H:3 * H], 0.5, None, ALU.mult).then_inc(lam_args, 1)
            om, em1, den, q1, q2 = (col(k) for k in range(15, 20))
            dve.wait_ge(act_param, 4)
            step(dve.tensor_scalar(om, tanh, -1.0, 1.0, ALU.mult, ALU.add))
            step(dve.reciprocal(om, om))
            step(dve.scalar_tensor_tensor(em1, tanh, 2.0, om, ALU.mult, ALU.mult))
            step(dve.tensor_tensor(q1, are, are, ALU.mult))
            step(dve.tensor_tensor(q2, aim, aim, ALU.mult))
            step(dve.tensor_tensor(den, q1, q2, ALU.add))
            step(dve.reciprocal(den, den))
            s_own, s_cross, s_th, s_half = (args[:, k * H:(k + 1) * H] for k in range(4))
            sq, cosm, nr, ni = (col(k) for k in range(20, 24))
            dve.wait_ge(act_param, 5)
            step(dve.tensor_tensor(sq, s_half, s_half, ALU.mult))
            step(dve.tensor_scalar(cosm, sq, -2.0, 1.0, ALU.mult, ALU.add))
            step(dve.tensor_tensor(q1, em1, cosm, ALU.mult))
            step(dve.scalar_tensor_tensor(nr, sq, -2.0, q1, ALU.mult, ALU.add))
            step(dve.scalar_tensor_tensor(ni, em1, 1.0, s_th, ALU.add, ALU.mult))
            step(dve.tensor_tensor(q1, nr, are, ALU.mult))
            step(dve.tensor_tensor(q2, ni, aim, ALU.mult))
            step(dve.tensor_tensor(q1, q1, q2, ALU.add))
            step(dve.tensor_tensor(q2, ni, are, ALU.mult))
            step(dve.tensor_tensor(sq, nr, aim, ALU.mult))
            step(dve.tensor_tensor(q2, q2, sq, ALU.subtract))
            step(dve.scalar_tensor_tensor(q1, q1, 2.0, den, ALU.mult, ALU.mult))
            step(dve.scalar_tensor_tensor(q2, q2, 2.0, den, ALU.mult, ALU.mult))
            step(dve.tensor_tensor(nr, cr, q1, ALU.mult))
            step(dve.tensor_tensor(ni, ci, q2, ALU.mult))
            step(dve.tensor_tensor(nr, nr, ni, ALU.subtract))
            step(dve.tensor_tensor(ni, cr, q2, ALU.mult))
            step(dve.tensor_tensor(sq, ci, q1, ALU.mult))
            step(dve.tensor_tensor(ni, ni, sq, ALU.add))
            dve.tensor_copy(coef[0:N, :, 0], nr[0:N, :]).then_inc(coef_ready, 1)
            dve.tensor_copy(coef[0:N, :, 1], ni[0:N, :]).then_inc(coef_ready, 1)
            dve.tensor_copy(coef[N:P, :, 0], ni[N:P, :]).then_inc(coef_ready, 1)
            dve.tensor_scalar(coef[N:P, :, 1], nr[N:P, :], -1.0, None, ALU.mult).then_inc(coef_ready, 1)
            powers(0, 0, first=True)
            step(dve.tensor_tensor(lam_own[:], s_own, eq, ALU.mult))
            step(dve.tensor_tensor(lam_cross[:], s_cross, eq, ALU.mult))
            dve.tensor_tensor(mask[:], cst[:, C_LPOS:C_LPOS + ND].unsqueeze(2).to_broadcast([P, ND, B]),
                              len_sb[:].unsqueeze(1).to_broadcast([P, ND, B]), ALU.is_lt).then_inc(masked, 2)
            dve.wait_ge(masked, 2)
            whole(1)
            sum_k(0, first=True)

            def between_first(d):
                if d == 0:
                    k_rows(0, first=True)
                if d == 4:
                    powers(1, 1, first=True)
            scan(0, 0, between_first)
            whole(2)

            with dve.Fori(0, 3) as i:
                for u in range(2):
                    g = i * 2 + u
                    sum_k(g + 1)

                    def between(d):
                        if d == 0:
                            k_rows(g + 1)
                        if 1 <= d <= YQ:
                            mask_y(g, d - 1)
                        if d == YQ:
                            powers(g + 2, u)
                    scan(g + 1, 1 - u, between)
                    whole(g + 3)
            sum_k(7)

            def between_last(d):
                if d == 0:
                    k_rows(7)
                if 1 <= d <= YQ:
                    mask_y(6, d - 1)
            scan(7, 1, between_last)
            for r in range(YQ):
                mask_y(7, r)

            dve.wait_ge(added, 2 + NG * YQ)
            for u in range(2):
                dve.memset(h_stk[u][3 * 32:KB, :].bitcast(F32), 1.0).then_inc(dve_step, 1)
                count[0] += 1
            dve.wait_ge(in_bias, 16)
            rows = slice(3 * 32, KB)
            hi = b_stk[0][rows, :]
            step(dve.tensor_copy(hi, bias[rows, :]))
            step(dve.tensor_tensor(bias_t[rows, :], bias[rows, :], hi.bitcast(F32), ALU.subtract))
            step(dve.tensor_scalar(bias[rows, :], hi.bitcast(F32), cst[rows, C_SEL:C_SEL + 1], None, ALU.mult))
            for u in range(2):
                step(dve.scalar_tensor_tensor(b_stk[u][rows, :], bias_t[rows, :], cst[rows, C_SEL + 1:C_SEL + 2],
                                              bias[rows, :], ALU.mult, ALU.add))

            def low_x(t, u):
                dve.wait_ge(xs_hi_ready, t + 1)
                src = x[:].rearrange("p h (d b) -> p d b h", b=B)
                for k in range(2):
                    ins = dve.tensor_tensor(xs_lo[u][:, :, k * H:(k + 1) * H],
                                            src[:, :, bass.ds(t * 2 + k, 1), :].rearrange("p d b h -> p d (b h)"),
                                            xs_hi[u][:, :, k * H:(k + 1) * H].bitcast(F32), ALU.subtract)
                ins.then_inc(xs_lo_ready, 1)

            def low_a(t, u):
                dve.wait_ge(a_hi_ready, t + 1)
                dve.tensor_tensor(a_lo[u][:].rearrange("p c (k r) -> p c k r", k=2),
                                  a_raw[u][:].rearrange("p k (c r) -> p c k r", r=R),
                                  a_hi[u][:].bitcast(F32).rearrange("p c (k r) -> p c k r", k=2),
                                  ALU.subtract).then_inc(a_lo_ready, 1)

            def stack_b(t, u, i):
                dve.wait_ge(in_b[u], i * 32 + 32)
                dve.wait_ge(out_ready, t * 2 + 2)
                dve.tensor_copy(b_stk[u][0:32, :], b_raw[u][:]).then_inc(b_hi_ready, 1)
                dve.tensor_copy(b_stk[u][32:64, :], b_raw[u][:]).then_inc(b_hi_ready, 1)
                dve.wait_ge(b_hi_ready, t * 2 + 2)
                dve.tensor_tensor(b_stk[u][64:96, :], b_raw[u][:], b_stk[u][0:32, :].bitcast(F32),
                                  ALU.subtract).then_inc(b_ready, 1)

            def stack_h(t, u):
                dve.wait_ge(h_ready, t + 1)
                hp = psY[0:2 * R, u, 0:P]
                own = cst[0:2 * R, C_BM:C_BM + P]
                dve.tensor_tensor(h_f32[:], hp, own, ALU.mult).then_inc(h_step, 1)
                dve.tensor_tensor(h_stk[u][0:32, :], hp, own, ALU.mult).then_inc(h_step, 1)
                dve.tensor_tensor(h_stk[u][64:96, :], hp, own, ALU.mult).then_inc(h_step, 1)
                dve.wait_ge(h_step, t * 4 + 3)
                dve.tensor_tensor(h_stk[u][32:64, :], h_f32[:], h_stk[u][0:32, :].bitcast(F32),
                                  ALU.subtract).then_inc(h_step, 1)

            low_x(0, 0)
            low_a(0, 0)
            stack_b(0, 0, 0)
            with dve.Fori(0, NT // 2 - 1) as i:
                for u in range(2):
                    t = i * 2 + u
                    stack_h(t, u)
                    low_x(t + 1, 1 - u)
                    low_a(t + 1, 1 - u)
                    stack_b(t + 1, 1 - u, i + u)
            stack_h(NT - 2, 0)
            low_x(NT - 1, 1)
            low_a(NT - 1, 1)
            stack_b(NT - 1, 1, NT // 2 - 1)
            stack_h(NT - 1, 1)

        @block.gpsimd
        def _(pool):
            def fraction(q):
                pool.wait_ge(whole_ready, q + 1)
                pool.tensor_tensor(phase[:], turn[:], phase[:], ALU.subtract).then_inc(frac_ready, 1)

            def magnitude(q):
                if not (isinstance(q, int) and q == 0):
                    pool.wait_ge(exps_ready, q * 2)
                else:
                    pool.wait_ge(modes_ready, 1)
                t = modes[:, bass.ds(q * G, G), :]
                pool.tensor_tensor(mag[:].rearrange("p c (m n) -> p c m n", m=MA),
                                   t[:, :, MB:MB + MA].unsqueeze(3).to_broadcast([P, G, MA, MB]),
                                   t[:, :, 0:MB].unsqueeze(2).to_broadcast([P, G, MA, MB]),
                                   ALU.mult).then_inc(mag_ready, 1)

            def rotation(q):
                if not (isinstance(q, int) and q == 0):
                    pool.wait_ge(v_made, q * 2)
                else:
                    pool.wait_ge(coef_ready, 4)
                pool.tensor_tensor(rot[:].rearrange("p c a n -> p (c a) n"),
                                   cst[:, C_M2:C_M2 + N].unsqueeze(1).to_broadcast([P, 2 * G, N]),
                                   coef[:, bass.ds(q * G, G), :].rearrange("p c a -> p (c a)").unsqueeze(2)
                                   .to_broadcast([P, 2 * G, N]), ALU.mult).then_inc(rot_ready, 1)

            def eye_w(g):
                pool.wait_ge(in_w, g * 16 + 16)
                d = w_raw[:, bass.ds(g * Q, Q)]
                pool.tensor_tensor(d, d, cst[:, C_EYE:C_EYE + P], ALU.add).then_inc(w_eye, 1)

            def low_w(g):
                pool.wait_ge(w_hi_ready, g + 1)
                pool.tensor_tensor(w_lo[:, bass.ds(g, 1), :].rearrange("p c o -> p (c o)"), w_raw[:],
                                   w_hi[:, bass.ds(g, 1), :].rearrange("p c o -> p (c o)").bitcast(F32),
                                   ALU.subtract).then_inc(w_lo_ready, 1)

            def add_y(g, r):
                pool.wait_ge(masked, g * YQ + r + 3)
                d = x[:, bass.ds(g * G + 2 * r, 2), :]
                pool.tensor_tensor(d, d, ym[r % 2][:], ALU.add).then_inc(added, 1)

            def weights_and_sums(g):
                eye_w(g)
                add_y(g, 0)
                add_y(g, 1)
                low_w(g)
                add_y(g, 2)
                add_y(g, 3)

            pool.memset(credit[0:1, 0:1], 0.0).then_inc(added, 2)
            pool.memset(credit[0:1, 1:2], 0.0).then_inc(out_ready, 4)
            pool.memset(credit[0:1, 2:3], 0.0).then_inc(out_taken, 4)
            pool.memset(credit[0:1, 3:4], 0.0).then_inc(out_stored[0], 16)
            pool.memset(credit[0:1, 4:5], 0.0).then_inc(out_stored[1], 16)
            pool.wait_ge(in_small, 80)
            for q in range(2):
                fraction(q)
                magnitude(q)
                rotation(q)
            with pool.Fori(0, 3) as i:
                for u in range(2):
                    g = i * 2 + u
                    fraction(g + 2)
                    magnitude(g + 2)
                    rotation(g + 2)
                    weights_and_sums(g)
            weights_and_sums(6)
            weights_and_sums(7)


def kernel(**inputs):
    import numpy as np
    import concourse.bacc as bacc
    from concourse.bass_utils import run_bass_kernel_spmd

    a = {k: np.asarray(v) for k, v in inputs.items()}
    both = lambda m: np.concatenate([m, m], axis=0)
    ld = np.broadcast_to(a["L0_cond_log_dt"][None, :], (P, H))
    c = a["L0_cond_C"]
    arrays = {
        "xT": np.ascontiguousarray(a["x"].reshape(B, H, ND, Q).transpose(3, 1, 2, 0).reshape(Q, H, ND * B)),
        "par": np.ascontiguousarray(np.stack(
            [ld, both(a["L0_cond_log_A_real"].T), both(a["L0_cond_A_imag"].T),
             both(c[:, :, 0].T), both(c[:, :, 1].T)], axis=1)),
        "dvec": np.ascontiguousarray(a["L0_cond_D"].reshape(NG, G).T),
        "lens": np.ascontiguousarray(np.broadcast_to(a["itok_B_78_3631"][None, :], (P, B))),
        "slots": np.ascontiguousarray(a["itok_B_0_23"][None, :]),
        "wT": np.ascontiguousarray(a["L1_cond_W"].T.reshape(ND, Q, L).transpose(1, 0, 2)),
        "bias2": np.ascontiguousarray(np.broadcast_to(a["L1_cond_b"][None, :], (2, L))),
        "loraA": np.ascontiguousarray(a["L1_cond_lora_As"].reshape(SLOTS, ND, Q, R).transpose(0, 2, 1, 3)
                                      .reshape(SLOTS, Q, ND * R)),
        "loraB": np.ascontiguousarray(a["L1_cond_lora_Bs"]),
        "consts": constants(),
    }
    nc = bacc.Bacc("TRN2", target_bir_lowering=False, num_devices=1)
    args = [nc.dram_tensor(n, v.shape, mybir.dt.from_np(v.dtype), kind="ExternalInput").ap()
            for n, v in arrays.items()]
    out = nc.dram_tensor("out", (B * H, L), F32, kind="ExternalOutput").ap()
    conv_then_lora(nc, *args, out)
    r = run_bass_kernel_spmd(nc, [arrays], core_ids=[0])
    return r.results[0]["out"].reshape(B, H, L)
```

```python
from contextlib import ExitStack

import concourse.bass as bass
from concourse import mybir

ALU = mybir.AluOpType
ACT = mybir.ActivationFunctionType
AX_X = mybir.AxisListType.X
F32 = mybir.dt.float32
F32R = mybir.dt.float32r
I32 = mybir.dt.int32

P = 128
B, H, L = 32, 64, 1024
N = 64
Q = 128
ND = L // Q
G = 8
NG = H // G
R = 16
SLOTS = 32
NT = B // 2
WARM = 20
PI = 3.141592653589793
TWO_PI = 6.2831850
ROUND = 12582912.0
LOG2E = 1.4426950408889634
LN2_HI = 0.693359375
LN2_LO = -2.12194440e-4

NJ = Q + 1
MA, MB = 8, 16
C_J, C_EYE, C_REV, C_M2, C_OFF, C_OFFX, C_LPOS, C_EXP, C_BM, C_SEL, C_END = (
    0, 129, 257, 385, 449, 450, 451, 459, 483, 611, 613)


def constants():
    import numpy as np
    c = np.zeros((P, C_END), np.float32)
    p = np.arange(P)
    c[:, C_J:C_J + NJ] = Q - np.arange(NJ)
    c[:, C_EYE:C_EYE + P] = np.eye(P)
    c[:, C_REV:C_REV + P] = np.eye(P)[::-1]
    c[:, C_M2:C_M2 + N] = (p[:, None] % N == np.arange(N)[None, :])
    c[:, C_OFF] = np.where(p < N, 0.25, 0.5)
    c[:, C_OFFX] = np.where(p < N, 0.0, 0.5)
    c[:, C_LPOS:C_LPOS + ND] = p[:, None] + Q * np.arange(ND)[None, :]
    c[:, C_EXP:C_EXP + MB] = MB - np.arange(MB)
    c[:, C_EXP + MB:C_EXP + MB + MA] = MB * (MA - 1 - np.arange(MA))
    c[:2 * R, C_BM:C_BM + P] = 2.0 * (p[:2 * R, None] // R == np.arange(P)[None, :] // H)
    c[3 * 32, C_SEL] = 1.0
    c[3 * 32 + 1, C_SEL + 1] = 1.0
    return c


def conv_then_lora(nc, xT, xB, par, dvec, lens, slots, wT, bias2, loraA, loraB, consts, out):
    kpad = nc.dram_tensor("kpad", [2, G, 2 * Q], F32, kind="Internal").ap()

    with ExitStack() as ctx:
        def sb(name, shape, dt=F32, stack=ctx):
            return stack.enter_context(nc.sbuf_tensor(name, shape, dt))

        def sem(name):
            return ctx.enter_context(nc.semaphore(name))

        x = sb("x", [P, H, ND * B])
        w_hi = sb("w_hi", [P, ND, L], F32R)
        before = ExitStack()
        w_raw = sb("w_raw", [P, ND, L], stack=before)
        before.close()
        w_lo = sb("w_lo", [P, ND, L], F32R)
        cst = sb("cst", [P, C_END])
        slot_ids = sb("slot_ids", [1, B], I32)
        credit = sb("credit", [1, 8])
        mask = sb("mask", [P, ND, B])
        one = ExitStack()
        modes = sb("modes", [P, H + G, MB + MA], stack=one)
        mag = sb("mag", [P, G, NJ], stack=one)
        turn = sb("turn", [P, G, NJ], stack=one)
        phase = sb("phase", [P, G, NJ], stack=one)
        exps_rev = sb("exps_rev", [P, G, NJ], stack=one)
        vin = sb("vin", [P, G, P], stack=one)
        rot = sb("rot", [P, G, 2, N], stack=one)
        hank = sb("hank", [P, G, Q], stack=one)
        exps, toep, st = [], [], []
        for u in range(2):
            exps.append(sb(f"exps{u}", [P, G, Q], stack=one))
            toep.append(sb(f"toep{u}", [P, G, Q], stack=one))
            st.append(sb(f"st{u}", [P, G, ND - 1, B], stack=one))
        sa = sb("sa", [P, G, B], stack=one)
        sx = sb("sx", [P, G, B], stack=one)
        prm = exps[1][:].rearrange("p g j -> p (g j)")[:, 0:5 * H].rearrange("p (k h) -> p k h", k=5)
        freq = sb("freq", [P, H + G], stack=one)
        lam_own = sb("lam_own", [P, H], stack=one)
        lam_cross = sb("lam_cross", [P, H], stack=one)
        coef = sb("coef", [P, H + G, 2], stack=one)
        len_sb = sb("len_sb", [P, B], I32, stack=one)
        d_sb = sb("d_sb", [G, NG], stack=one)
        kcol = sb("kcol", [P, G], stack=one)
        krow = sb("krow", [G, Q], stack=one)
        zero = hank[0:2 * G, 0, :]
        one.close()
        two = ExitStack()
        KB = 3 * 32 + 2
        a_raw = [sb(f"a_raw{u}", [P, 2, P], stack=two) for u in range(2)]
        b_raw = [sb(f"b_raw{u}", [2 * R, L], stack=two) for u in range(2)]
        xt = [sb(f"xt{u}", [P, ND, 2, H], stack=two) for u in range(2)]
        a_hi = [sb(f"a_hi{u}", [P, ND, 2 * R], F32R, stack=two) for u in range(2)]
        a_lo = [sb(f"a_lo{u}", [P, ND, 2 * R], F32R, stack=two) for u in range(2)]
        h_f32 = sb("h_f32", [2 * R, P], stack=two)
        h_stk = [sb(f"h_stk{u}", [KB, P], F32R, stack=two) for u in range(2)]
        bias = sb("bias", [KB, L], stack=two)
        b_stk = [sb(f"b_stk{u}", [KB, L], F32R, stack=two) for u in range(2)]
        bias_t = sb("bias_t", [KB, L], stack=two)
        zt = sb("zt", [P, ND, 2, H], stack=two)
        xs_hi, xs_lo = [], []
        for u in range(2):
            xs_hi.append(sb(f"xs_hi{u}", [P, ND, P], F32R, stack=two))
            xs_lo.append(sb(f"xs_lo{u}", [P, ND, P], F32R, stack=two))
        res = [sb(f"res{u}", [P, L], stack=two) for u in range(2)]
        two.close()

        psU = ctx.enter_context(nc.psum_tensor("psU", [P, G, 256], F32))
        psY = ctx.enter_context(nc.psum_tensor("psY", [P, 2, 512], F32))
        psV = ctx.enter_context(nc.psum_tensor("psV", [P, 2, 512], F32))

        in_par = sem("in_par")
        in_small = sem("in_small")
        in_x = [sem(f"in_x{u}") for u in range(2)]
        in_w = sem("in_w")
        zeros_made = sem("zeros_made")
        zeros_stored = sem("zeros_stored")
        k_stored = sem("k_stored")
        hankel_in = sem("hankel_in")
        flipped = sem("flipped")
        toep_ready = sem("toep_ready")
        dve_step = sem("dve_step")
        rates_ready = sem("rates_ready")
        act_param = sem("act_param")
        freq_ready = sem("freq_ready")
        lam_args = sem("lam_args")
        lam_ready = sem("lam_ready")
        turn_ready = sem("turn_ready")
        whole_ready = sem("whole_ready")
        frac_ready = sem("frac_ready")
        sin_ready = sem("sin_ready")
        modes_ready = sem("modes_ready")
        mag_ready = sem("mag_ready")
        coef_ready = sem("coef_ready")
        rot_ready = sem("rot_ready")
        exps_ready = sem("exps_ready")
        fwd_ready = sem("fwd_ready")
        v_made = sem("v_made")
        v_ready = sem("v_ready")
        u_ready = sem("u_ready")
        kcol_ready = sem("kcol_ready")
        k_turned = sem("k_turned")
        krow_ready = sem("krow_ready")
        scan_step = sem("scan_step")
        crossed = sem("crossed")
        u_copied = sem("u_copied")
        pool_step = sem("pool_step")
        two_c = sem("two_c")
        y_ready = sem("y_ready")
        y_taken = sem("y_taken")
        mask_ready = sem("mask_ready")
        w_eye = sem("w_eye")
        w_hi_ready = sem("w_hi_ready")
        w_lo_ready = sem("w_lo_ready")
        in_a = [sem(f"in_a{u}") for u in range(2)]
        in_b = [sem(f"in_b{u}") for u in range(2)]
        in_bias = sem("in_bias")
        in_xt = [sem(f"in_xt{u}") for u in range(2)]
        z_masked = sem("z_masked")
        x1_ready = sem("x1_ready")
        x1_first = sem("x1_first")
        first_hi = sem("first_hi")
        first_masked = sem("first_masked")
        xs_hi_ready = sem("xs_hi_ready")
        xs_lo_ready = sem("xs_lo_ready")
        a_hi_ready = sem("a_hi_ready")
        a_lo_ready = sem("a_lo_ready")
        b_hi_ready = sem("b_hi_ready")
        b_ready = sem("b_ready")
        h_ready = sem("h_ready")
        h_step = sem("h_step")
        out_ready = sem("out_ready")
        out_taken = sem("out_taken")
        out_stored = [sem(f"out_stored{u}") for u in range(2)]

        STEPS = 5 * (ND - 2)
        HELPED = ND - 2
        EARLY = H - G
        YQ = G // 2

        def scan_base(q):
            return 0 if isinstance(q, int) and q == 0 else q * STEPS - HELPED

        def wait_layer1(eng):
            eng.wait_ge(y_taken, 2 + NG * YQ)

        def fraction(eng, q):
            eng.wait_ge(whole_ready, q + 1)
            eng.tensor_tensor(phase[:], turn[:], phase[:], ALU.subtract).then_inc(frac_ready, 1)

        def powers(eng, q, half):
            eng.wait_ge(sin_ready, q + 1)
            eng.wait_ge(mag_ready, q + 2)
            if not (isinstance(q, int) and q == 0):
                eng.wait_ge(v_made, q * 2 - 2 + half + 1)
                eng.wait_ge(fwd_ready, q * 2 - 2 + half + 1)
            rows = slice(4 * half, 4 * half + 4)
            eng.tensor_tensor(exps_rev[:, rows, :], phase[:, rows, :], mag[:, rows, :],
                              ALU.mult).then_inc(exps_ready, 1)

        block = ctx.enter_context(nc.Block())

        @block.sync
        def _(sp):
            def load_x(g, u):
                sp.dma_start(x[:, bass.ds(g * G, G), :], xT[:, bass.ds(g * G, G), :]).then_inc(in_x[u], 16)

            def load_w(g):
                sp.dma_start(w_raw[:, bass.ds(g, 1), :], wT[:, bass.ds(g, 1), :]).then_inc(in_w, 16)

            def hankel(q, u, first=False):
                sp.wait_ge(krow_ready, q * 2 + 2)
                sp.dma_start(kpad[u, :, Q:2 * Q], krow[:]).then_inc(k_stored, 16)
                sp.wait_ge(k_stored, q * 16 + 16)
                if not first:
                    sp.wait_ge(flipped, q * 2)
                src = bass.AP(tensor=kpad.tensor, offset=u * G * 2 * Q + 1, ap=[[1, P], [2 * Q, G], [1, Q]])
                sp.dma_start(hank[:], src).then_inc(hankel_in, 16)

            sp.dma_start(prm, par).then_inc(in_par, 16)
            sp.dma_start(len_sb[:], lens).then_inc(in_small, 16)
            sp.dma_start(d_sb[:], dvec).then_inc(in_small, 16)
            sp.dma_start(slot_ids[:], slots).then_inc(in_small, 16)
            load_x(0, 0)
            sp.wait_ge(zeros_made, 1)
            sp.dma_start(kpad[:, :, 0:Q].rearrange("u c q -> (u c) q"), zero).then_inc(zeros_stored, 16)
            load_x(1, 1)
            load_w(0)
            sp.wait_ge(zeros_stored, 16)
            hankel(0, 0, first=True)

            def group(g, u, i, more_x=True):
                if more_x:
                    sp.wait_ge(in_x[u], i * 16 + 16)
                    load_x(g + 2, u)
                sp.wait_ge(in_w, g * 16 + 16)
                load_w(g + 1)
                hankel(g + 1, 1 - u)

            with sp.Fori(0, 3) as i:
                for u in range(2):
                    group(i * 2 + u, u, i)
            group(6, 0, 3, more_x=False)

            def load_xt(t, u):
                sp.dma_start(xt[u][:].rearrange("p d b h -> p (d b h)"), xB[bass.ds(t * P, P), :]).then_inc(in_xt[u], 16)

            def load_ab(t, u):
                for k in range(2):
                    s = sp.value_load(slot_ids[0:1, bass.ds(t * 2 + k, 1)], min_val=0, max_val=SLOTS - 1)
                    sp.dma_start(a_raw[u][:, k, :],
                                 loraA[bass.ds(s, 1)].rearrange("s p f -> (s p) f")).then_inc(in_a[u], 16)
                    sp.dma_start(b_raw[u][R * k:R * k + R, :],
                                 loraB[bass.ds(s, 1)].rearrange("s r f -> (s r) f")).then_inc(in_b[u], 16)

            sp.wait_ge(mag_ready, NG + 2)
            sp.wait_ge(sin_ready, NG + 1)
            for u in range(2):
                load_xt(u, u)
                load_ab(u, u)
            sp.wait_ge(rot_ready, NG + 1)
            sp.wait_ge(u_ready, 2 * NG)
            sp.wait_ge(kcol_ready, NG)
            sp.dma_start(bias[3 * 32:KB, :], bias2).then_inc(in_bias, 16)

            def tile(t, u, last=False):
                if not last:
                    sp.wait_ge(a_lo_ready, t + 1)
                    sp.wait_ge(b_ready, t + 1)
                    load_ab(t + 2, u)
                    sp.wait_ge(xs_lo_ready, t + 1)
                    load_xt(t + 2, u)
                for half in range(2):
                    sp.wait_ge(out_taken, t * 2 + 4 + half + 1)
                    cols = slice(512 * half, 512 * half + 512)
                    sp.dma_start(out[bass.ds(t * P, P), cols], res[u][:, cols]).then_inc(out_stored[u], 16)

            with sp.Fori(0, NT // 2 - 1) as i:
                for u in range(2):
                    tile(i * 2 + u, u)
            for u in range(2):
                tile(NT - 2 + u, u, last=True)
            for u in range(2):
                sp.wait_ge(out_stored[u], 32 * (NT // 2 + 1))

        @block.tensor
        def _(pe):
            def make_v(q):
                pe.wait_ge(rot_ready, q + 1)
                for half in range(2):
                    pe.wait_ge(exps_ready, q * 2 + half + 1)
                    if not isinstance(q, int):
                        pe.wait_ge(toep_ready, q * 2 - 2 + half + 1)
                    elif q == 1:
                        pe.wait_ge(v_ready, half + 1)
                        if half == 0:
                            pe.wait_ge(krow_ready, 2)
                    for k in range(4):
                        c = 4 * half + k
                        mm = pe.matmul(psV[:, half, k * P:(k + 1) * P], exps_rev[:, c, 1:NJ],
                                       rot[:, c, :, :].rearrange("p a n -> p (a n)"), start=True, stop=True)
                    mm.then_inc(v_made, 1)

            def inject(q, u, i):
                pe.wait_ge(in_x[u], i * 16 + 16)
                for half in range(2):
                    pe.wait_ge(v_ready, q * 2 + half + 1)
                    if not (isinstance(q, int) and q == 0):
                        pe.wait_ge(u_copied, q * 2 - 2 + half + 1)
                    for k in range(4):
                        c = 4 * half + k
                        mm = pe.matmul(psU[:, c, 0:(ND - 1) * B], vin[:, c, :],
                                       x[:, bass.ds(q * G + c, 1), 0:(ND - 1) * B].rearrange("p a f -> p (a f)"),
                                       start=True, stop=True)
                    mm.then_inc(u_ready, 1)

            def turn_k(q):
                pe.wait_ge(kcol_ready, q + 1)
                if isinstance(q, int) and q == 1:
                    pe.wait_ge(toep_ready, 1)
                pe.matmul(psV[0:G, 0, 0:Q], kcol[:], cst[:, C_REV:C_REV + Q],
                          start=True, stop=True).then_inc(k_turned, 1)

            def flip(q):
                pe.wait_ge(hankel_in, q * 16 + 16)
                for half in range(2):
                    if isinstance(q, int) and q == 0:
                        pe.wait_ge(v_ready, 2 + half + 1)
                    pe.matmul(psV[:, half, :], cst[:, C_REV:C_REV + Q],
                              hank[:, 4 * half:4 * half + 4, :].rearrange("p c j -> p (c j)"),
                              start=True, stop=True).then_inc(flipped, 1)

            def outputs(g, u):
                pe.wait_ge(toep_ready, g * 2 + 2)
                pe.wait_ge(fwd_ready, g * 2 + 2)
                for r in range(YQ):
                    pe.wait_ge(y_taken, g * YQ + r + 1)
                    for k in range(2):
                        c = 2 * r + k
                        pe.matmul(psY[:, r % 2, k * 256:(k + 1) * 256], toep[u][:, c, :],
                                  x[:, bass.ds(g * G + c, 1), :].rearrange("p a f -> p (a f)"),
                                  start=True, stop=False)
                        if c == 0:
                            pe.wait_ge(scan_step, scan_base(g) + STEPS - (HELPED if isinstance(g, int) and g == NG - 1 else 0)
                                       if not (isinstance(g, int) and g == 0) else STEPS - HELPED)
                        mm = pe.matmul(psY[:, r % 2, k * 256 + B:(k + 1) * 256], exps[u][:, c, :],
                                       st[u][:, c, :, :].rearrange("p d b -> p (d b)"), start=False, stop=True)
                    mm.then_inc(y_ready, 1)

            pe.wait_ge(in_small, 64)
            pe.wait_ge(lam_args, 1)
            for _ in range(WARM):
                pe.matmul(psV[:, 0, 0:256], cst[:, C_EYE:C_EYE + P], cst[:, 0:256], start=True, stop=True)
            make_v(0)
            inject(0, 0, 0)
            turn_k(0)
            make_v(1)
            inject(1, 1, 0)
            flip(0)
            turn_k(1)
            with pe.Fori(0, 3) as i:
                for u in range(2):
                    g = i * 2 + u
                    outputs(g, u)
                    flip(g + 1)
                    make_v(g + 2)
                    inject(g + 2, u, i + 1)
                    turn_k(g + 2)
            outputs(6, 0)
            flip(7)
            outputs(7, 1)

            def tile(t, u):
                acc = psU[:, 4 * u:4 * u + 4, :].rearrange("p a f -> p (a f)")
                hp = psY[0:2 * R, u, 0:P]
                pe.wait_ge(xs_lo_ready, t + 1)
                pe.wait_ge(a_lo_ready, t + 1)
                n = 0
                for c in range(ND):
                    for a, v in ((a_hi, xs_hi), (a_lo, xs_hi), (a_hi, xs_lo)):
                        mm = pe.matmul(hp, a[u][:, c, :], v[u][:, c, :],
                                       start=(n == 0), stop=(n == 3 * ND - 1))
                        n += 1
                mm.then_inc(h_ready, 1)
                pe.wait_ge(w_lo_ready, NG)
                pe.wait_ge(out_taken, t * 2 + 2)
                for half in range(2):
                    cols = slice(512 * half, 512 * half + 512)
                    for c in range(ND):
                        for v, w in ((xs_hi, w_hi), (xs_hi, w_lo), (xs_lo, w_hi)):
                            pe.matmul(acc[:, cols], v[u][:, c, :], w[:, c, cols],
                                      start=(c == 0 and w is w_hi and v is xs_hi), stop=False)
                    if half == 0:
                        pe.wait_ge(h_step, t * 4 + 4)
                        pe.wait_ge(b_ready, t + 1)
                    pe.matmul(acc[:, cols], h_stk[u][:, :], b_stk[u][:, cols],
                              start=False, stop=True).then_inc(out_ready, 1)

            with pe.Fori(0, NT // 2) as i:
                for u in range(2):
                    tile(i * 2 + u, u)

        @block.scalar
        def _(act):
            def turns(q, part=range(G)):
                act.wait_ge(frac_ready, q)
                for c in part:
                    a = act.activation(turn[:, c, :], cst[:, C_J:C_J + NJ], ACT.Identity,
                                       bias=cst[:, C_OFF:C_OFF + 1], scale=freq[:, bass.ds(q * G + c, 1)])
                if c == G - 1:
                    a.then_inc(turn_ready, 1)

            def sines(q):
                act.wait_ge(frac_ready, q + 1)
                act.activation(phase[:], phase[:], ACT.Sin, scale=TWO_PI).then_inc(sin_ready, 1)

            def forward(q, u):
                for half in range(2):
                    act.wait_ge(exps_ready, q * 2 + half + 1)
                    if half == 0 and not isinstance(q, int):
                        act.wait_ge(y_ready, q * YQ - YQ)
                    rows = slice(4 * half, 4 * half + 4)
                    act.activation(exps[u][:, rows, :], exps_rev[:, rows, Q - 1::-1],
                                   ACT.Copy).then_inc(fwd_ready, 1)

            def copy_v(q):
                for half in range(2):
                    act.wait_ge(v_made, q * 2 + half + 1)
                    if not (isinstance(q, int) and q == 0):
                        act.wait_ge(u_ready, q * 2 - 2 + half + 1)
                        act.wait_ge(kcol_ready, q)
                    act.activation(vin[:, 4 * half:4 * half + 4, :].rearrange("p c s -> p (c s)"),
                                   psV[:, half, :], ACT.Copy).then_inc(v_ready, 1)

            def copy_u(q, u):
                for half in range(2):
                    act.wait_ge(u_ready, q * 2 + half + 1)
                    if half == 0 and not isinstance(q, int):
                        act.wait_ge(y_ready, q * YQ - YQ)
                    rows = slice(4 * half, 4 * half + 4)
                    act.activation(st[u][:, rows, :, :].rearrange("p c d b -> p c (d b)"),
                                   psU[:, rows, 0:(ND - 1) * B], ACT.Copy).then_inc(u_copied, 1)

            def k_rows(q):
                act.wait_ge(k_turned, q + 1)
                if not (isinstance(q, int) and q == 0):
                    act.wait_ge(k_stored, q * 16)
                act.activation(krow[:, 1:Q], psV[0:G, 0, 1:Q], ACT.Copy).then_inc(krow_ready, 1)
                act.activation(krow[:, 0:1], psV[0:G, 0, 0:1], ACT.Identity,
                               bias=d_sb[:, bass.ds(q, 1)]).then_inc(krow_ready, 1)

            def copy_toep(q, u, half):
                act.wait_ge(flipped, q * 2 + half + 1)
                if half == 0 and not (isinstance(q, int) and q < 2):
                    act.wait_ge(y_ready, q * YQ - YQ)
                act.activation(toep[u][:, 4 * half:4 * half + 4, :].rearrange("p c j -> p (c j)"),
                               psV[:, half, :], ACT.Copy).then_inc(toep_ready, 1)

            def split_w(g):
                act.wait_ge(w_eye, g + 1)
                act.activation(w_hi[:, bass.ds(g, 1), :], w_raw[:, bass.ds(g, 1), :],
                               ACT.Copy).then_inc(w_hi_ready, 1)

            def take_y(g, r):
                act.wait_ge(y_ready, g * YQ + r + 1)
                act.activation(x[:, bass.ds(g * G + 2 * r, 2), :],
                               psY[:, r % 2, :].rearrange("p (a f) -> p a f", a=2), ACT.Copy).then_inc(y_taken, 1)

            act.dma_start(cst[:], consts).then_inc(in_small, 16)
            tmp = st[1][:].rearrange("p g d b -> p (g d b)")
            act.wait_ge(rates_ready, 2)
            act.activation(tmp[:, 4 * H:5 * H], tmp[:, 2 * H:3 * H], ACT.Tanh, scale=0.5).then_inc(act_param, 1)
            act.activation(tmp[:, 5 * H:6 * H], tmp[:, 2 * H:3 * H], ACT.Exp, scale=float(Q)).then_inc(act_param, 1)
            act.wait_ge(lam_args, 1)
            act.activation(modes[:, 0:H, :], modes[:, 0:H, :], ACT.Exp).then_inc(modes_ready, 1)
            act.wait_ge(lam_args, 2)
            act.activation(tmp[:, 8 * H:12 * H], tmp[:, 8 * H:12 * H], ACT.Sin, scale=TWO_PI).then_inc(act_param, 1)
            sines(0)
            turns(1)
            forward(0, 0)
            sines(1)
            copy_v(0)
            copy_u(0, 0)
            k_rows(0)
            sines(2)
            forward(1, 1)
            copy_v(1)
            copy_u(1, 1)
            for half in range(2):
                copy_toep(0, 0, half)

            with act.Fori(0, 3) as i:
                for u in range(2):
                    g = i * 2 + u
                    k_rows(g + 1)
                    split_w(g)
                    turns(g + 3, range(0, 1))
                    take_y(g, 0)
                    turns(g + 3, range(1, 4))
                    take_y(g, 1)
                    turns(g + 3, range(4, 7))
                    take_y(g, 2)
                    turns(g + 3, range(7, 8))
                    take_y(g, 3)
                    for half in range(2):
                        copy_toep(g + 1, 1 - u, half)
                    copy_v(g + 2)
                    sines(g + 3)
                    forward(g + 2, u)
                    copy_u(g + 2, u)
            k_rows(7)
            split_w(6)
            for r in range(YQ):
                take_y(6, r)
            for half in range(2):
                copy_toep(7, 1, half)
            split_w(7)
            take_y(7, 0)

            def split_x(t, u):
                act.wait_ge(out_ready, t * 2 + 2)
                act.wait_ge(x1_ready, t)
                act.activation(xs_hi[u][:].rearrange("p d f -> p (d f)"),
                               xt[u][:].rearrange("p d b h -> p (d b h)"), ACT.Copy).then_inc(xs_hi_ready, 1)

            def split_a(t, u, i):
                act.wait_ge(in_a[u], i * 32 + 32)
                act.activation(a_hi[u][:].rearrange("p c (k r) -> p c k r", k=2),
                               a_raw[u][:].rearrange("p k (c r) -> p c k r", r=R), ACT.Copy).then_inc(a_hi_ready, 1)

            def take(t, u, i):
                for half in range(2):
                    act.wait_ge(out_ready, t * 2 + 4 + half + 1)
                    if half == 0:
                        act.wait_ge(out_stored[u], i * 32 + 32)
                    act.activation(res[u][:, 512 * half:512 * half + 512],
                                   psU[:, 4 * u + 2 * half:4 * u + 2 * half + 2, :].rearrange("p a f -> p (a f)"),
                                   ACT.Copy).then_inc(out_taken, 1)

            def split_first(rows, count):
                act.wait_ge(x1_first, count)
                act.activation(xs_hi[0][:].rearrange("p d (b h) -> p d b h", b=2)[:, :, :, rows],
                               xt[0][:, :, :, rows], ACT.Copy).then_inc(first_hi, 1)

            split_a(0, 0, 0)
            take_y(7, 1)
            split_first(slice(0, EARLY), 1)
            take_y(7, 2)
            take_y(7, 3)
            split_first(slice(EARLY, H), 2)
            with act.Fori(0, NT // 2 - 1) as i:
                for u in range(2):
                    t = i * 2 + u
                    split_x(t + 1, 1 - u)
                    split_a(t + 1, 1 - u, i + u)
                    take(t, u, i)
            split_x(NT - 1, 1)
            split_a(NT - 1, 1, NT // 2 - 1)
            take(NT - 2, 0, NT // 2 - 1)
            take(NT - 1, 1, NT // 2 - 1)

        @block.vector
        def _(dve):
            count = [0]

            def step(ins):
                mark(ins)
                dve.wait_ge(dve_step, count[0])

            def mark(ins):
                count[0] += 1
                ins.then_inc(dve_step, 1)

            tmp = st[1][:].rearrange("p g d b -> p (g d b)")

            def col(k, n=1):
                return tmp[:, k * H:(k + n) * H]

            def whole(q):
                dve.wait_ge(turn_ready, q + 1)
                if not (isinstance(q, int) and q == 0):
                    dve.wait_ge(exps_ready, q * 2)
                dve.tensor_scalar(phase[:], turn[:], ROUND, -ROUND, ALU.add, ALU.add).then_inc(whole_ready, 1)

            def sum_k(q):
                dve.wait_ge(v_ready, q * 2 + 2)
                if not (isinstance(q, int) and q == 0):
                    dve.wait_ge(k_turned, q)
                dve.tensor_reduce(kcol[:], vin[:, :, 0:N], AX_X, ALU.add).then_inc(kcol_ready, 1)

            def scan(q, u, fillers, helped=False):
                base = scan_base(q)
                size = 4 if helped else 5
                fillers = list(fillers)

                def fill():
                    piece = fillers.pop(0) if fillers else None
                    if piece:
                        piece[0](*piece[1:])

                s = st[u]
                own = lam_own[:, bass.ds(q * G, G)].unsqueeze(2).to_broadcast([P, G, B])
                cross = lam_cross[:, bass.ds(q * G, G)].unsqueeze(2).to_broadcast([P, G, B])
                dve.wait_ge(u_copied, q * 2 + 2)
                if not (isinstance(q, int) and q == 0):
                    dve.wait_ge(scan_step, base)
                for d in range(1, ND - 1):
                    done = base + size * (d - 1)
                    if d > 1:
                        fill()
                        dve.wait_ge(scan_step, done)
                    dve.tensor_tensor(sa[:], s[:, :, d - 1, :], own, ALU.mult).then_inc(scan_step, 1)
                    dve.tensor_tensor(sx[0:N], s[N:P, :, d - 1, :], cross[N:P], ALU.mult).then_inc(scan_step, 1)
                    if not helped:
                        dve.tensor_tensor(sx[N:P], s[0:N, :, d - 1, :], cross[0:N], ALU.mult).then_inc(scan_step, 1)
                    dve.wait_ge(scan_step, done + 1)
                    dve.tensor_tensor(s[:, :, d, :], s[:, :, d, :], sa[:], ALU.add).then_inc(scan_step, 1)
                    fill()
                    dve.wait_ge(scan_step, done + size - 1)
                    if helped:
                        dve.wait_ge(crossed, (HELPED if q else 0) + d)
                    dve.tensor_tensor(s[:, :, d, :], s[:, :, d, :], sx[:], ALU.add).then_inc(scan_step, 1)
                while fillers:
                    fill()

            dt, ea, decay, theta, tanh, eq = (col(k) for k in range(6))
            are, args = col(6), col(8, 4)
            cr, ci, aim = prm[:, 3, :], prm[:, 4, :], prm[:, 2, :]
            dve.memset(zero, 0.0).then_inc(zeros_made, 1)
            dve.memset(mag[:, :, Q:NJ], 1.0).then_inc(mag_ready, 1)
            mark(dve.memset(modes[:, H:H + G, :], 0.0))
            mark(dve.memset(coef[:, H:H + G, :], 0.0))
            step(dve.memset(freq[:, H:H + G], 0.0))
            logs = prm[:, 0:2, :].rearrange("p k h -> p (k h)")
            k2, r2, q2_, p2 = col(12, 2), col(14, 2), col(16, 2), col(18, 2)
            dve.wait_ge(in_par, 16)
            step(dve.tensor_scalar(k2, logs, LOG2E, ROUND, ALU.mult, ALU.add))
            step(dve.tensor_scalar(k2, k2, -ROUND, -126.0, ALU.add, ALU.max))
            step(dve.scalar_tensor_tensor(r2, k2, -LN2_HI, logs, ALU.mult, ALU.add))
            step(dve.scalar_tensor_tensor(r2, k2, -LN2_LO, r2, ALU.mult, ALU.add))
            mark(dve.tensor_scalar(p2.bitcast(I32), k2, 127.0, 8388608.0, ALU.add, ALU.mult))
            step(dve.tensor_scalar(q2_, r2, 1.0 / 5040, 1.0 / 720, ALU.mult, ALU.add))
            step(dve.tensor_tensor(q2_, q2_, r2, ALU.mult))
            for c in (1.0 / 120, 1.0 / 24, 1.0 / 6, 0.5, 1.0):
                step(dve.scalar_tensor_tensor(q2_, q2_, c, r2, ALU.add, ALU.mult))
            step(dve.scalar_tensor_tensor(col(0, 2), q2_, 1.0, p2, ALU.add, ALU.mult))
            dve.tensor_tensor(theta, aim, dt, ALU.mult).then_inc(rates_ready, 1)
            dve.scalar_tensor_tensor(decay, ea, -1.0, dt, ALU.mult, ALU.mult).then_inc(rates_ready, 1)
            dve.wait_ge(rates_ready, 2)
            dve.tensor_scalar(freq[:, 0:H], theta, 1.0 / (2 * PI), None, ALU.mult).then_inc(freq_ready, 1)
            dve.tensor_scalar(are, ea, -1.0, None, ALU.mult).then_inc(freq_ready, 1)
            dve.wait_ge(in_small, 64)
            jm = cst[:, C_EXP:C_EXP + MA + MB].unsqueeze(1).to_broadcast([P, H, MA + MB])
            dve.tensor_tensor(modes[:, 0:H, :], decay.unsqueeze(2).to_broadcast([P, H, MA + MB]), jm,
                              ALU.mult).then_inc(lam_args, 1)
            dve.wait_ge(freq_ready, 2)
            f = freq[:, 0:H]
            mark(dve.tensor_scalar(args[:, 0:H], f, float(Q), 0.25, ALU.mult, ALU.add))
            mark(dve.tensor_scalar(args[:, H:2 * H], f, float(Q), cst[:, C_OFFX:C_OFFX + 1], ALU.mult, ALU.add))
            step(dve.tensor_copy(args[:, 2 * H:3 * H], f))
            wh = col(12, 3)
            step(dve.tensor_scalar(wh, args[:, 0:3 * H], ROUND, -ROUND, ALU.add, ALU.add))
            step(dve.tensor_tensor(args[:, 0:3 * H], args[:, 0:3 * H], wh, ALU.subtract))
            dve.tensor_scalar(args[:, 3 * H:4 * H], args[:, 2 * H:3 * H], 0.5, None, ALU.mult).then_inc(lam_args, 1)
            om, em1 = col(15), col(16)
            dve.wait_ge(act_param, 1)
            step(dve.tensor_scalar(om, tanh, -1.0, 1.0, ALU.mult, ALU.add))
            step(dve.reciprocal(om, om))
            step(dve.scalar_tensor_tensor(em1, tanh, 2.0, om, ALU.mult, ALU.mult))
            whole(0)
            fraction(dve, 0)
            den, wr, wi = col(22), col(24), col(26)
            dve.wait_ge(two_c, 3)
            step(dve.reciprocal(den, den))
            mark(dve.scalar_tensor_tensor(wr, wr, 2.0, den, ALU.mult, ALU.mult))
            mark(dve.scalar_tensor_tensor(wi, wi, 2.0, den, ALU.mult, ALU.mult))
            s_own, s_cross, s_th, s_half = (args[:, k * H:(k + 1) * H] for k in range(4))
            sq, cosm, nr, ni, m1, m2, m3, m4 = (col(k) for k in (20, 21, 12, 13, 14, 15, 17, 18))
            dve.wait_ge(act_param, 3)
            mark(dve.tensor_tensor(sq, s_half, s_half, ALU.mult))
            step(dve.scalar_tensor_tensor(ni, em1, 1.0, s_th, ALU.add, ALU.mult))
            step(dve.tensor_scalar(cosm, sq, -2.0, 1.0, ALU.mult, ALU.add))
            step(dve.tensor_tensor(cosm, em1, cosm, ALU.mult))
            step(dve.scalar_tensor_tensor(nr, sq, -2.0, cosm, ALU.mult, ALU.add))
            mark(dve.tensor_tensor(m1, nr, wr, ALU.mult))
            mark(dve.tensor_tensor(m2, ni, wi, ALU.mult))
            mark(dve.tensor_tensor(m3, nr, wi, ALU.mult))
            step(dve.tensor_tensor(m4, ni, wr, ALU.mult))
            dve.tensor_tensor(coef[0:N, 0:H, 0], m1[0:N, :], m2[0:N, :], ALU.subtract).then_inc(coef_ready, 1)
            dve.tensor_tensor(coef[0:N, 0:H, 1], m3[0:N, :], m4[0:N, :], ALU.add).then_inc(coef_ready, 1)
            dve.tensor_tensor(coef[N:P, 0:H, 0], m3[N:P, :], m4[N:P, :], ALU.add).then_inc(coef_ready, 1)
            dve.tensor_tensor(coef[N:P, 0:H, 1], m2[N:P, :], m1[N:P, :], ALU.subtract).then_inc(coef_ready, 1)
            powers(dve, 0, 0)
            powers(dve, 0, 1)
            dve.tensor_tensor(lam_own[:], s_own, eq, ALU.mult).then_inc(lam_ready, 1)
            dve.tensor_tensor(lam_cross[:], s_cross, eq, ALU.mult).then_inc(lam_ready, 1)
            dve.tensor_tensor(mask[:], cst[:, C_LPOS:C_LPOS + ND].unsqueeze(2).to_broadcast([P, ND, B]),
                              len_sb[:].unsqueeze(1).to_broadcast([P, ND, B]), ALU.is_lt).then_inc(mask_ready, 1)
            whole(1)
            fraction(dve, 1)
            powers(dve, 1, 0)
            powers(dve, 1, 1)
            sum_k(0)
            whole(2)
            fraction(dve, 2)
            dve.wait_ge(lam_ready, 2)
            scan(0, 0, [None, None, None, None, None, (sum_k, 1)], helped=True)

            with dve.Fori(0, 3) as i:
                for u in range(2):
                    g = i * 2 + u
                    scan(g + 1, 1 - u, [None] * 5 + [(whole, g + 3)])
                    sum_k(g + 2)
            scan(7, 1, [], helped=True)

            def x1_early(rows, n, taken):
                dve.wait_ge(y_taken, taken)
                z = x[:].rearrange("p h (d b) -> p d b h", b=B)[:, :, 0:2, rows]
                m = mask[:, :, 0:2].unsqueeze(3).to_broadcast([P, ND, 2, rows.stop - rows.start])
                dve.tensor_tensor(zt[:, :, :, rows], z, m, ALU.mult).then_inc(first_masked, 1)
                dve.wait_ge(in_xt[0], 16)
                dve.wait_ge(first_masked, n)
                dve.tensor_tensor(xt[0][:, :, :, rows], xt[0][:, :, :, rows], zt[:, :, :, rows],
                                  ALU.add).then_inc(x1_first, 1)

            def low_early(rows, n, last=False):
                dve.wait_ge(first_hi, n)
                ins = dve.tensor_tensor(xs_lo[0][:].rearrange("p d (b h) -> p d b h", b=2)[:, :, :, rows],
                                        xt[0][:, :, :, rows],
                                        xs_hi[0][:].bitcast(F32).rearrange("p d (b h) -> p d b h", b=2)[:, :, :, rows],
                                        ALU.subtract)
                if last:
                    ins.then_inc(xs_lo_ready, 1)

            def make_x1(t, u, i):
                z = x[:].rearrange("p h (d b) -> p d b h", b=B)[:, :, bass.ds(t * 2, 2), :]
                m = mask[:, :, bass.ds(t * 2, 2)].unsqueeze(3).to_broadcast([P, ND, 2, H])
                dve.tensor_tensor(zt[:], z, m, ALU.mult).then_inc(z_masked, 1)
                dve.wait_ge(in_xt[u], i * 16 + 16)
                dve.wait_ge(z_masked, t)
                dve.tensor_tensor(xt[u][:].rearrange("p d b h -> p (d b h)"),
                                  xt[u][:].rearrange("p d b h -> p (d b h)"),
                                  zt[:].rearrange("p d b h -> p (d b h)"), ALU.add).then_inc(x1_ready, 1)

            def low_x(t, u):
                dve.wait_ge(xs_hi_ready, t)
                dve.tensor_tensor(xs_lo[u][:].rearrange("p d f -> p (d f)"),
                                  xt[u][:].rearrange("p d b h -> p (d b h)"),
                                  xs_hi[u][:].rearrange("p d f -> p (d f)").bitcast(F32),
                                  ALU.subtract).then_inc(xs_lo_ready, 1)

            def low_a(t, u):
                dve.wait_ge(a_hi_ready, t + 1)
                dve.tensor_tensor(a_lo[u][:].rearrange("p c (k r) -> p c k r", k=2),
                                  a_raw[u][:].rearrange("p k (c r) -> p c k r", r=R),
                                  a_hi[u][:].bitcast(F32).rearrange("p c (k r) -> p c k r", k=2),
                                  ALU.subtract).then_inc(a_lo_ready, 1)

            def stack_b(t, u, i):
                dve.wait_ge(in_b[u], i * 32 + 32)
                dve.wait_ge(out_ready, t * 2 + 2)
                dve.tensor_copy(b_stk[u][0:32, :], b_raw[u][:]).then_inc(b_hi_ready, 1)
                dve.tensor_copy(b_stk[u][32:64, :], b_raw[u][:]).then_inc(b_hi_ready, 1)
                dve.wait_ge(b_hi_ready, t * 2 + 2)
                dve.tensor_tensor(b_stk[u][64:96, :], b_raw[u][:], b_stk[u][0:32, :].bitcast(F32),
                                  ALU.subtract).then_inc(b_ready, 1)

            def stack_h(t, u):
                dve.wait_ge(h_ready, t + 1)
                hp = psY[0:2 * R, u, 0:P]
                own = cst[0:2 * R, C_BM:C_BM + P]
                dve.tensor_tensor(h_f32[:], hp, own, ALU.mult).then_inc(h_step, 1)
                dve.tensor_tensor(h_stk[u][0:32, :], hp, own, ALU.mult).then_inc(h_step, 1)
                dve.tensor_tensor(h_stk[u][64:96, :], hp, own, ALU.mult).then_inc(h_step, 1)
                dve.wait_ge(h_step, t * 4 + 3)
                dve.tensor_tensor(h_stk[u][32:64, :], h_f32[:], h_stk[u][0:32, :].bitcast(F32),
                                  ALU.subtract).then_inc(h_step, 1)

            x1_early(slice(0, EARLY), 1, 2 + (NG - 1) * YQ)
            for u in range(2):
                mark(dve.memset(h_stk[u][3 * 32:KB, :].bitcast(F32), 1.0))
            dve.wait_ge(in_bias, 16)
            rows = slice(3 * 32, KB)
            hi = b_stk[0][rows, :]
            dve.wait_ge(flipped, 2 * NG)
            step(dve.tensor_copy(hi, bias[rows, :]))
            step(dve.tensor_tensor(bias_t[rows, :], bias[rows, :], hi.bitcast(F32), ALU.subtract))
            step(dve.tensor_scalar(bias[rows, :], hi.bitcast(F32), cst[rows, C_SEL:C_SEL + 1], None, ALU.mult))
            for u in range(2):
                step(dve.scalar_tensor_tensor(b_stk[u][rows, :], bias_t[rows, :], cst[rows, C_SEL + 1:C_SEL + 2],
                                              bias[rows, :], ALU.mult, ALU.add))
            low_early(slice(0, EARLY), 1)
            low_a(0, 0)
            x1_early(slice(EARLY, H), 2, 2 + NG * YQ)
            low_early(slice(EARLY, H), 2, last=True)
            stack_b(0, 0, 0)
            make_x1(1, 1, 0)
            with dve.Fori(0, NT // 2 - 1) as i:
                for u in range(2):
                    t = i * 2 + u
                    stack_h(t, u)
                    low_x(t + 1, 1 - u)
                    low_a(t + 1, 1 - u)
                    stack_b(t + 1, 1 - u, i + u)
                    make_x1(t + 2, u, i + 1)
            stack_h(NT - 2, 0)
            low_x(NT - 1, 1)
            low_a(NT - 1, 1)
            stack_b(NT - 1, 1, NT // 2 - 1)
            stack_h(NT - 1, 1)

        @block.gpsimd
        def _(pool):
            def magnitude(q):
                if not (isinstance(q, int) and q == 0):
                    pool.wait_ge(exps_ready, q * 2)
                else:
                    pool.wait_ge(modes_ready, 1)
                t = modes[:, bass.ds(q * G, G), :]
                pool.tensor_tensor(mag[:, :, 0:Q].rearrange("p c (m n) -> p c m n", m=MA),
                                   t[:, :, MB:MB + MA].unsqueeze(3).to_broadcast([P, G, MA, MB]),
                                   t[:, :, 0:MB].unsqueeze(2).to_broadcast([P, G, MA, MB]),
                                   ALU.mult).then_inc(mag_ready, 1)

            def rotation(q):
                if not (isinstance(q, int) and q == 0):
                    pool.wait_ge(v_made, q * 2)
                else:
                    pool.wait_ge(coef_ready, 4)
                pool.tensor_tensor(rot[:].rearrange("p c a n -> p (c a) n"),
                                   cst[:, C_M2:C_M2 + N].unsqueeze(1).to_broadcast([P, 2 * G, N]),
                                   coef[:, bass.ds(q * G, G), :].rearrange("p c a -> p (c a)").unsqueeze(2)
                                   .to_broadcast([P, 2 * G, N]), ALU.mult).then_inc(rot_ready, 1)

            def eye_w(g):
                pool.wait_ge(in_w, g * 16 + 16)
                d = w_raw[:, bass.ds(g, 1), bass.ds(g * Q, Q)]
                pool.tensor_tensor(d, d, cst[:, C_EYE:C_EYE + P].unsqueeze(1), ALU.add).then_inc(w_eye, 1)

            def low_w(g):
                pool.wait_ge(w_hi_ready, g + 1)
                pool.tensor_tensor(w_lo[:, bass.ds(g, 1), :], w_raw[:, bass.ds(g, 1), :], w_hi[:, bass.ds(g, 1), :].bitcast(F32),
                                   ALU.subtract).then_inc(w_lo_ready, 1)

            pool.memset(credit[0:1, 0:1], 0.0).then_inc(y_taken, 2)
            pool.memset(credit[0:1, 1:2], 0.0).then_inc(out_ready, 4)
            pool.memset(credit[0:1, 2:3], 0.0).then_inc(out_taken, 4)
            pool.memset(credit[0:1, 3:4], 0.0).then_inc(out_stored[0], 32)
            pool.memset(credit[0:1, 4:5], 0.0).then_inc(out_stored[1], 32)
            tmp = st[1][:].rearrange("p g d b -> p (g d b)")

            def first_turns(q):
                for c in range(G):
                    ins = pool.tensor_scalar(turn[:, c, :], cst[:, C_J:C_J + NJ], freq[:, q * G + c:q * G + c + 1],
                                             cst[:, C_OFF:C_OFF + 1], ALU.mult, ALU.add)
                ins.then_inc(turn_ready, 1)

            def help_scan(q, u):
                pool.wait_ge(lam_ready, 2)
                pool.wait_ge(u_copied, q * 2 + 2)
                cross = lam_cross[0:N, q * G:q * G + G].unsqueeze(2).to_broadcast([N, G, B])
                for d in range(1, ND - 1):
                    if scan_base(q) + 4 * (d - 1) > 0:
                        pool.wait_ge(scan_step, scan_base(q) + 4 * (d - 1))
                    pool.tensor_tensor(sx[N:P], st[u][0:N, :, d - 1, :], cross, ALU.mult).then_inc(crossed, 1)

            pool.wait_ge(in_small, 64)
            pool.wait_ge(freq_ready, 2)
            first_turns(0)

            def col(k):
                return tmp[:, k * H:(k + 1) * H]
            are, aim, cr, ci = col(6), prm[:, 2, :], prm[:, 3, :], prm[:, 4, :]
            for n, (o, a, b) in enumerate(((22, are, are), (23, aim, aim), (24, cr, are), (25, ci, aim),
                                           (26, ci, are), (27, cr, aim))):
                pool.tensor_tensor(col(o), a, b, ALU.mult).then_inc(pool_step, 1)
            pool.wait_ge(pool_step, 6)
            pool.tensor_tensor(col(22), col(22), col(23), ALU.add).then_inc(two_c, 1)
            pool.tensor_tensor(col(24), col(24), col(25), ALU.add).then_inc(two_c, 1)
            pool.tensor_tensor(col(26), col(26), col(27), ALU.subtract).then_inc(two_c, 1)
            magnitude(0)
            rotation(0)
            magnitude(1)
            pool.wait_ge(frac_ready, 2)
            first_turns(2)
            eye_w(0)
            rotation(1)
            pool.wait_ge(rot_ready, 2)
            help_scan(0, 0)
            pool.wait_ge(crossed, HELPED)
            magnitude(2)
            rotation(2)
            with pool.Fori(0, 3) as i:
                for u in range(2):
                    g = i * 2 + u
                    powers(pool, g + 2, 0)
                    powers(pool, g + 2, 1)
                    magnitude(g + 3)
                    low_w(g)
                    fraction(pool, g + 3)
                    eye_w(g + 1)
                    rotation(g + 3)
            eye_w(7)
            pool.wait_ge(w_eye, NG)
            help_scan(7, 1)
            pool.wait_ge(crossed, 2 * HELPED)
            low_w(6)
            low_w(7)


def kernel(**inputs):
    import numpy as np
    import concourse.bacc as bacc
    from concourse.bass_utils import run_bass_kernel_spmd

    a = {k: np.asarray(v) for k, v in inputs.items()}
    both = lambda m: np.concatenate([m, m], axis=0)
    ld = np.broadcast_to(a["L0_cond_log_dt"][None, :], (P, H))
    c = a["L0_cond_C"]
    arrays = {
        "xT": np.ascontiguousarray(a["x"].reshape(B, H, ND, Q).transpose(3, 1, 2, 0).reshape(Q, H, ND * B)),
        "xB": np.ascontiguousarray(a["x"].reshape(NT, 2, H, ND, Q).transpose(0, 4, 3, 1, 2)
                                   .reshape(NT * Q, ND * 2 * H)),
        "par": np.ascontiguousarray(np.stack(
            [ld, both(a["L0_cond_log_A_real"].T), both(a["L0_cond_A_imag"].T),
             both(c[:, :, 0].T), both(c[:, :, 1].T)], axis=1)),
        "dvec": np.ascontiguousarray(a["L0_cond_D"].reshape(NG, G).T),
        "lens": np.ascontiguousarray(np.broadcast_to(a["itok_B_78_3631"][None, :], (P, B))),
        "slots": np.ascontiguousarray(a["itok_B_0_23"][None, :]),
        "wT": np.ascontiguousarray(a["L1_cond_W"].T.reshape(ND, Q, L).transpose(1, 0, 2)),
        "bias2": np.ascontiguousarray(np.broadcast_to(a["L1_cond_b"][None, :], (2, L))),
        "loraA": np.ascontiguousarray(a["L1_cond_lora_As"].reshape(SLOTS, ND, Q, R).transpose(0, 2, 1, 3)
                                      .reshape(SLOTS, Q, ND * R)),
        "loraB": np.ascontiguousarray(a["L1_cond_lora_Bs"]),
        "consts": constants(),
    }
    nc = bacc.Bacc("TRN2", target_bir_lowering=False, num_devices=1)
    args = [nc.dram_tensor(n, v.shape, mybir.dt.from_np(v.dtype), kind="ExternalInput").ap()
            for n, v in arrays.items()]
    out = nc.dram_tensor("out", (B * H, L), F32, kind="ExternalOutput").ap()
    conv_then_lora(nc, *args, out)
    r = run_bass_kernel_spmd(nc, [arrays], core_ids=[0])
    return r.results[0]["out"].reshape(B, H, L)
```

```python
from contextlib import ExitStack

import concourse.bass as bass
from concourse import mybir

ALU = mybir.AluOpType
ACT = mybir.ActivationFunctionType
F32 = mybir.dt.float32
F32R = mybir.dt.float32r
I32 = mybir.dt.int32

P = 128
B, H, L = 32, 64, 1024
N = 64
Q = 128
ND = L // Q
G = 8
NG = H // G
R = 16
SLOTS = 32
NT = B // 2
WARM = 12
PI = 3.141592653589793
TWO_PI = 6.2831850
ROUND = 12582912.0
LOG2E = 1.4426950408889634
LN2_HI = 0.693359375
LN2_LO = -2.12194440e-4

NJ = Q + 1
MA, MB = 8, 16
C_J, C_EYE, C_M2, C_OFF, C_OFFX, C_LPOS, C_EXP, C_BM, C_SEL, C_END = (
    0, 129, 257, 321, 322, 323, 331, 355, 483, 485)


def constants():
    import numpy as np
    c = np.zeros((P, C_END), np.float32)
    p = np.arange(P)
    c[:, C_J:C_J + NJ] = np.arange(NJ)
    c[:, C_EYE:C_EYE + P] = np.eye(P)
    c[:, C_M2:C_M2 + N] = (p[:, None] % N == np.arange(N)[None, :])
    c[:, C_OFF] = np.where(p < N, 0.25, 0.5)
    c[:, C_OFFX] = np.where(p < N, 0.0, 0.5)
    c[:, C_LPOS:C_LPOS + ND] = p[:, None] + Q * np.arange(ND)[None, :]
    c[:, C_EXP:C_EXP + MB] = 1 + np.arange(MB)
    c[:, C_EXP + MB:C_EXP + MB + MA] = MB * np.arange(MA)
    c[:2 * R, C_BM:C_BM + P] = 2.0 * (p[:2 * R, None] // R == np.arange(P)[None, :] // H)
    c[3 * 32, C_SEL] = 1.0
    c[3 * 32 + 1, C_SEL] = -1.0
    c[3 * 32 + 1, C_SEL + 1] = 1.0
    return c


def conv_then_lora(nc, xT, xB, par, dvec, lens, slots, wT, bias2, loraA, loraB, consts, out):
    kpad = nc.dram_tensor("kpad", [2, G, 2 * Q], F32, kind="Internal").ap()

    with ExitStack() as ctx:
        def sb(name, shape, dt=F32, stack=ctx):
            return stack.enter_context(nc.sbuf_tensor(name, shape, dt))

        def sem(name):
            return ctx.enter_context(nc.semaphore(name))

        x = sb("x", [P, H, ND * B])
        early = ExitStack()
        scratch = sb("scratch", [P, ND, L], stack=early)
        early.close()
        w_hi = sb("w_hi", [P, ND, L], F32R)
        before = ExitStack()
        w_raw = sb("w_raw", [P, ND, L], stack=before)
        before.close()
        w_lo = sb("w_lo", [P, ND, L], F32R)
        cst = sb("cst", [P, C_END])
        slot_ids = sb("slot_ids", [1, B], I32)
        credit = sb("credit", [1, 8])
        mask = sb("mask", [P, ND, B])
        KB = 3 * 32 + 2
        ones_rows = slice(3 * 32, KB)
        b_stk = [sb(f"b_stk{u}", [KB, L], F32R) for u in range(2)]
        h_stk = [sb(f"h_stk{u}", [KB, P], F32R) for u in range(2)]
        bias_in, bias_hi = scratch[ones_rows, ND - 1, :], scratch[ones_rows, ND - 2, :]
        one = ExitStack()
        modes = sb("modes", [P, H + G, MB + MA], stack=one)
        mag = sb("mag", [P, G, NJ], stack=one)
        turn = sb("turn", [P, G, NJ], stack=one)
        phase = sb("phase", [P, G, NJ], stack=one)
        pows = sb("pows", [P, G, NJ], stack=one)
        vin = sb("vin", [P, G, P], stack=one)
        rot = sb("rot", [P, G, 2, N], stack=one)
        exps, toep, st = [], [], []

        def group_buffers(u):
            exps.append(sb(f"exps{u}", [P, G, Q], stack=one))
            toep.append(sb(f"toep{u}", [P, G, Q], stack=one))
            st.append(sb(f"st{u}", [P, G, ND - 1, B], stack=one))

        group_buffers(0)
        sa = sb("sa", [P, G, B], stack=one)
        sx = sb("sx", [P, G, B], stack=one)
        freq = sb("freq", [P, H + G], stack=one)
        lam_own = sb("lam_own", [P, H], stack=one)
        lam_cross = sb("lam_cross", [P, H], stack=one)
        coef = sb("coef", [P, H + G, 2], stack=one)
        len_sb = sb("len_sb", [P, B], I32, stack=one)
        d_sb = sb("d_sb", [P, NG, 2], stack=one)
        coef_re = sb("coef_re", [P, G], stack=one)
        krow = sb("krow", [P, 2, Q], stack=one)
        group_buffers(1)
        prm = exps[1][:].rearrange("p g j -> p (g j)")[:, 0:5 * H].rearrange("p (k h) -> p k h", k=5)
        zero = toep[1][0:2 * G, 0, :]
        one.close()
        two = ExitStack()
        a_raw = [sb(f"a_raw{u}", [P, 2, P], stack=two) for u in range(2)]
        b_raw = [sb(f"b_raw{u}", [2 * R, L], stack=two) for u in range(2)]
        xt = [sb(f"xt{u}", [P, ND, 2, H], stack=two) for u in range(2)]
        a_f = [sb(f"a_f{u}", [P, ND, 2 * R], stack=two) for u in range(2)]
        h_sum = sb("h_sum", [2 * R, P], stack=two)
        h_f32 = sb("h_f32", [2 * R, P], stack=two)
        zt = sb("zt", [P, ND, 2, H], stack=two)
        xs_hi, xs_lo = [], []
        for u in range(2):
            xs_hi.append(sb(f"xs_hi{u}", [P, ND, P], F32R, stack=two))
            xs_lo.append(sb(f"xs_lo{u}", [P, ND, P], F32R, stack=two))
        res = [sb(f"res{u}", [P, L], stack=two) for u in range(2)]
        two.close()

        psU = ctx.enter_context(nc.psum_tensor("psU", [P, G, 256], F32))
        psY = ctx.enter_context(nc.psum_tensor("psY", [P, 2, 512], F32))
        psV = ctx.enter_context(nc.psum_tensor("psV", [P, 2, 512], F32))

        in_par = sem("in_par")
        in_small = sem("in_small")
        in_x = [sem(f"in_x{u}") for u in range(2)]
        in_w = sem("in_w")
        zeros_made = sem("zeros_made")
        zeros_stored = sem("zeros_stored")
        k_stored = sem("k_stored")
        toep_ready = [sem(f"toep_ready{u}") for u in range(2)]
        dve_step = sem("dve_step")
        rates_ready = sem("rates_ready")
        act_param = sem("act_param")
        freq_ready = sem("freq_ready")
        lam_args = sem("lam_args")
        lam_ready = sem("lam_ready")
        turn_ready = sem("turn_ready")
        turn_half = sem("turn_half")
        whole_ready = sem("whole_ready")
        frac_ready = sem("frac_ready")
        sin_ready = sem("sin_ready")
        modes_ready = sem("modes_ready")
        mag_ready = sem("mag_ready")
        coef_ready = sem("coef_ready")
        rot_ready = sem("rot_ready")
        pows_ready = sem("pows_ready")
        e_ready = sem("e_ready")
        v_made = sem("v_made")
        v_ready = sem("v_ready")
        u_ready = sem("u_ready")
        k_made = sem("k_made")
        coef_re_ready = sem("coef_re_ready")
        krow_ready = sem("krow_ready")
        scan_step = sem("scan_step")
        crossed = sem("crossed")
        u_copied = sem("u_copied")
        pool_step = sem("pool_step")
        two_c = sem("two_c")
        y_ready = sem("y_ready")
        y_taken = sem("y_taken")
        mask_ready = sem("mask_ready")
        w_eye = sem("w_eye")
        w_hi_ready = sem("w_hi_ready")
        w_lo_ready = sem("w_lo_ready")
        in_a = [sem(f"in_a{u}") for u in range(2)]
        in_b = [sem(f"in_b{u}") for u in range(2)]
        in_bias = sem("in_bias")
        bias_step = sem("bias_step")
        ones_made = sem("ones_made")
        bias_ready = sem("bias_ready")
        in_xt = [sem(f"in_xt{u}") for u in range(2)]
        z_masked = sem("z_masked")
        x1_ready = sem("x1_ready")
        x1_first = sem("x1_first")
        first_hi = sem("first_hi")
        first_masked = sem("first_masked")
        xs_hi_ready = sem("xs_hi_ready")
        xs_lo_ready = sem("xs_lo_ready")
        a_ready = sem("a_ready")
        b_hi_ready = sem("b_hi_ready")
        b_ready = sem("b_ready")
        h_ready = sem("h_ready")
        h_step = sem("h_step")
        out_ready = sem("out_ready")
        out_taken = sem("out_taken")
        out_stored = [sem(f"out_stored{u}") for u in range(2)]

        STEPS = 5 * (ND - 2)
        HELPED = ND - 2
        CG = 4
        HS = CG + 4
        EARLY = H - G
        YQ = G // 2

        def k_bank(q):
            return psY[:, 0, 0:2 * Q] if isinstance(q, int) and q == 0 else psV[:, 0, 0:2 * Q]

        def scan_base(q):
            return 0 if isinstance(q, int) and q == 0 else q * STEPS - HELPED

        def scan_end(q):
            return scan_base(q) + STEPS - (HELPED if isinstance(q, int) and q in (0, NG - 1) else 0)

        def wait_layer1(eng):
            eng.wait_ge(y_taken, 2 + NG * YQ)

        def fraction(eng, q):
            eng.wait_ge(whole_ready, q + 1)
            eng.tensor_tensor(phase[:], turn[:], phase[:], ALU.subtract).then_inc(frac_ready, 1)

        def powers(eng, q, half):
            eng.wait_ge(sin_ready, q + 1)
            eng.wait_ge(mag_ready, q + 2)
            if not (isinstance(q, int) and q == 0):
                eng.wait_ge(v_made, q * 2 - 2 + half + 1)
                eng.wait_ge(e_ready, q * 2 - 2 + half + 1)
                eng.wait_ge(k_made, q)
            rows = slice(4 * half, 4 * half + 4)
            eng.tensor_tensor(pows[:, rows, :], phase[:, rows, :], mag[:, rows, :],
                              ALU.mult).then_inc(pows_ready, 1)

        def rotation(eng, q):
            if not (isinstance(q, int) and q == 0):
                eng.wait_ge(v_made, q * 2)
            else:
                eng.wait_ge(coef_ready, 4)
            eng.tensor_tensor(rot[:].rearrange("p c a n -> p (c a) n"),
                               cst[:, C_M2:C_M2 + N].unsqueeze(1).to_broadcast([P, 2 * G, N]),
                               coef[:, bass.ds(q * G, G), :].rearrange("p c a -> p (c a)").unsqueeze(2)
                               .to_broadcast([P, 2 * G, N]), ALU.mult).then_inc(rot_ready, 1)

        block = ctx.enter_context(nc.Block())

        @block.sync
        def _(sp):
            def load_x(g, u):
                sp.dma_start(x[:, bass.ds(g * G, G), :], xT[:, bass.ds(g * G, G), :]).then_inc(in_x[u], 16)

            def load_w(g):
                sp.dma_start(w_raw[:, bass.ds(g, 1), :], wT[:, bass.ds(g, 1), :]).then_inc(in_w, 16)

            def toeplitz(q, u):
                sp.wait_ge(krow_ready, q * 3 + 3)
                sp.dma_start(kpad[u, :, Q:2 * Q].rearrange("(s k) j -> k s j", s=2),
                             krow[0:P:32]).then_inc(k_stored, 16)
                sp.wait_ge(k_stored, q * 16 + 16)
                if not isinstance(q, int) or q > 1:
                    sp.wait_ge(y_ready, q * YQ - YQ)
                src = bass.AP(tensor=kpad.tensor, offset=u * G * 2 * Q + 1, ap=[[1, P], [2 * Q, G], [1, Q]])
                sp.dma_start(toep[u][:], src).then_inc(toep_ready[u], 16)

            sp.dma_start(prm, par).then_inc(in_par, 16)
            sp.dma_start(len_sb[:], lens).then_inc(in_small, 16)
            sp.dma_start(d_sb[:], dvec).then_inc(in_small, 16)
            sp.dma_start(slot_ids[:], slots).then_inc(in_small, 16)
            load_x(0, 0)
            sp.wait_ge(zeros_made, 1)
            sp.dma_start(kpad[:, :, 0:Q].rearrange("u c q -> (u c) q"), zero).then_inc(zeros_stored, 16)
            load_x(1, 1)
            load_w(0)
            sp.wait_ge(zeros_stored, 16)
            toeplitz(0, 0)

            def group(g, u, i, more_x=True):
                if more_x:
                    sp.wait_ge(in_x[u], i * 16 + 16)
                    load_x(g + 2, u)
                sp.wait_ge(in_w, g * 16 + 16)
                load_w(g + 1)
                toeplitz(g + 1, 1 - u)

            group(0, 0, 0)
            group(1, 1, 0)
            with sp.Fori(1, 3) as i:
                for u in range(2):
                    group(i * 2 + u, u, i)
            group(6, 0, 3, more_x=False)

            def load_xt(t, u):
                sp.dma_start(xt[u][:].rearrange("p d b h -> p (d b h)"), xB[bass.ds(t * P, P), :]).then_inc(in_xt[u], 16)

            def load_ab(t, u):
                for k in range(2):
                    s = sp.value_load(slot_ids[0:1, bass.ds(t * 2 + k, 1)], min_val=0, max_val=SLOTS - 1)
                    sp.dma_start(a_raw[u][:, k, :],
                                 loraA[bass.ds(s, 1)].rearrange("s p f -> (s p) f")).then_inc(in_a[u], 16)
                    sp.dma_start(b_raw[u][R * k:R * k + R, :],
                                 loraB[bass.ds(s, 1)].rearrange("s r f -> (s r) f")).then_inc(in_b[u], 16)

            sp.wait_ge(mag_ready, NG + 2)
            sp.wait_ge(sin_ready, NG + 1)
            for u in range(2):
                load_xt(u, u)
                load_ab(u, u)

            def tile(t, u, last=False):
                if not last:
                    sp.wait_ge(a_ready, t + 1)
                    sp.wait_ge(b_ready, t + 1)
                    load_ab(t + 2, u)
                    sp.wait_ge(h_ready, t + 1)
                    load_xt(t + 2, u)
                for half in range(2):
                    sp.wait_ge(out_taken, t * 2 + 4 + half + 1)
                    cols = slice(512 * half, 512 * half + 512)
                    sp.dma_start(out[bass.ds(t * P, P), cols], res[u][:, cols]).then_inc(out_stored[u], 16)

            with sp.Fori(0, NT // 2 - 1) as i:
                for u in range(2):
                    tile(i * 2 + u, u)
            for u in range(2):
                tile(NT - 2 + u, u, last=True)
            for u in range(2):
                sp.wait_ge(out_stored[u], 32 * (NT // 2 + 1))

        @block.tensor
        def _(pe):
            def make_v(q):
                pe.wait_ge(rot_ready, q + 1)
                for half in range(2):
                    pe.wait_ge(pows_ready, q * 2 + half + 1)
                    if not (isinstance(q, int) and q == 0):
                        pe.wait_ge(v_ready, q * 2 - 2 + half + 1)
                        if half == 0:
                            pe.wait_ge(krow_ready, q * 3)
                    for k in range(4):
                        c = 4 * half + k
                        mm = pe.matmul(psV[:, half, k * P:(k + 1) * P], pows[:, c, 0:Q],
                                       rot[:, c, :, :].rearrange("p a n -> p (a n)"), start=True, stop=True)
                    mm.then_inc(v_made, 1)

            def inject(q, u, i):
                pe.wait_ge(in_x[u], i * 16 + 16)
                for half in range(2):
                    pe.wait_ge(v_ready, q * 2 + half + 1)
                    if not (isinstance(q, int) and q == 0):
                        pe.wait_ge(u_copied, q * 2 - 2 + half + 1)
                    if isinstance(q, int) and q == 2 and half == 0:
                        pe.wait_ge(y_taken, 2 + YQ)
                    for k in range(4):
                        c = 4 * half + k
                        mm = pe.matmul(psU[:, c, 0:(ND - 1) * B], vin[:, c, :],
                                       x[:, bass.ds(q * G + c, 1), 0:(ND - 1) * B].rearrange("p a f -> p (a f)"),
                                       start=True, stop=True)
                    mm.then_inc(u_ready, 1)

            def make_k(q):
                pe.wait_ge(pows_ready, q * 2 + 2)
                if not (isinstance(q, int) and q == 0):
                    pe.wait_ge(v_ready, q * 2 + 1)
                pe.wait_ge(coef_re_ready, q + 1)
                for c in range(G):
                    k, slot = 32 * (c % 4), c // 4
                    mm = pe.matmul(k_bank(q)[k:k + 32, slot * Q:(slot + 1) * Q],
                                   coef_re[:, c:c + 1].to_broadcast([P, 32]),
                                   pows[:, c, 0:Q], start=True, stop=True)
                mm.then_inc(k_made, 1)

            def outputs_apart(g, u, i):
                pe.wait_ge(toep_ready[u], i * 16 + 16)
                pe.wait_ge(u_copied, 4 if g == 0 else 2 * NG)
                for c in range(G):
                    pe.matmul(psU[:, c, :], toep[u][:, c, :], x[:, g * G + c, :], start=(c % 2 == 0), stop=False)
                pe.wait_ge(e_ready, g * 2 + 2)
                pe.wait_ge(scan_step, scan_end(g))
                for c in range(G):
                    mm = pe.matmul(psU[:, c, B:256], exps[u][:, c, :],
                                   st[u][:, c, :, :].rearrange("p d b -> p (d b)"), start=False, stop=(c % 2 == 1))
                    if c % 2 == 1:
                        mm.then_inc(y_ready, 1)

            def outputs(g, u, i):
                for r in range(YQ):
                    pe.wait_ge(y_taken, g * YQ + r + 1)
                    for k in range(2):
                        c = 2 * r + k
                        if c == 0:
                            pe.wait_ge(toep_ready[u], i * 16 + 16)
                        pe.matmul(psY[:, r % 2, k * 256:(k + 1) * 256], toep[u][:, c, :],
                                  x[:, bass.ds(g * G + c, 1), :].rearrange("p a f -> p (a f)"),
                                  start=True, stop=False)
                        if c % 4 == 0:
                            pe.wait_ge(e_ready, g * 2 + c // 4 + 1)
                        if c == 0:
                            pe.wait_ge(scan_step, scan_end(g))
                        mm = pe.matmul(psY[:, r % 2, k * 256 + B:(k + 1) * 256], exps[u][:, c, :],
                                       st[u][:, c, :, :].rearrange("p d b -> p (d b)"), start=False, stop=True)
                    mm.then_inc(y_ready, 1)

            pe.wait_ge(in_small, 64)
            pe.wait_ge(lam_args, 1)
            for _ in range(WARM):
                pe.matmul(psV[:, 0, 0:256], cst[:, C_EYE:C_EYE + P], cst[:, 0:256], start=True, stop=True)
            make_k(0)
            make_v(0)
            inject(0, 0, 0)
            make_v(1)
            inject(1, 1, 0)
            make_k(1)

            def group(g, u, i):
                if isinstance(g, int) and g == 0:
                    outputs_apart(g, u, i)
                else:
                    outputs(g, u, i)
                make_v(g + 2)
                inject(g + 2, u, i + 1)
                make_k(g + 2)

            for u in range(2):
                group(u, u, 0)
            with pe.Fori(1, 3) as i:
                for u in range(2):
                    group(i * 2 + u, u, i)
            outputs(6, 0, 3)
            outputs_apart(7, 1, 3)

            pe.wait_ge(bias_ready, 2)
            pe.wait_ge(ones_made, 2)

            def tile(t, u):
                acc = psU[:, 4 * u:4 * u + 4, :].rearrange("p a f -> p (a f)")
                pe.wait_ge(xs_lo_ready, t + 1)
                pe.wait_ge(a_ready, t + 1)
                for c in range(ND):
                    k = c % CG
                    mm = pe.matmul(psY[32 * k:32 * k + 2 * R, u, 0:P], a_f[u][:, c, :],
                                   xt[u][:, c, :, :].rearrange("p b h -> p (b h)"),
                                   start=(c < CG), stop=(c >= ND - CG))
                mm.then_inc(h_ready, 1)
                pe.wait_ge(w_lo_ready, NG)
                pe.wait_ge(out_taken, t * 2 + 2)
                for half in range(2):
                    cols = slice(512 * half, 512 * half + 512)
                    for c in range(ND):
                        for v, w in ((xs_hi, w_hi), (xs_hi, w_lo), (xs_lo, w_hi)):
                            pe.matmul(acc[:, cols], v[u][:, c, :], w[:, c, cols],
                                      start=(c == 0 and w is w_hi and v is xs_hi), stop=False)
                    if half == 0:
                        pe.wait_ge(h_step, t * HS + HS)
                        pe.wait_ge(b_ready, t + 1)
                    pe.matmul(acc[:, cols], h_stk[u][:, :], b_stk[u][:, cols],
                              start=False, stop=True).then_inc(out_ready, 1)

            with pe.Fori(0, NT // 2) as i:
                for u in range(2):
                    tile(i * 2 + u, u)

        @block.scalar
        def _(act):
            def turns(q, part=range(G)):
                if isinstance(q, int) and q == 0:
                    act.wait_ge(in_small, 64)
                    act.wait_ge(freq_ready, 2)
                else:
                    act.wait_ge(frac_ready, q)
                for c in part:
                    a = act.activation(turn[:, c, :], cst[:, C_J:C_J + NJ], ACT.Identity,
                                       bias=cst[:, C_OFF:C_OFF + 1], scale=freq[:, bass.ds(q * G + c, 1)])
                if c == G - 1:
                    a.then_inc(turn_ready, 1)

            def sines(q):
                act.wait_ge(frac_ready, q + 1)
                act.activation(phase[:], phase[:], ACT.Sin, scale=TWO_PI).then_inc(sin_ready, 1)

            def copy_e(q, u):
                for half in range(2):
                    act.wait_ge(pows_ready, q * 2 + half + 1)
                    if half == 0 and not isinstance(q, int):
                        act.wait_ge(y_ready, q * YQ - YQ)
                    rows = slice(4 * half, 4 * half + 4)
                    act.activation(exps[u][:, rows, :], pows[:, rows, 1:NJ],
                                   ACT.Copy).then_inc(e_ready, 1)

            def copy_v(q):
                for half in range(2):
                    act.wait_ge(v_made, q * 2 + half + 1)
                    if not (isinstance(q, int) and q == 0):
                        act.wait_ge(u_ready, q * 2 - 2 + half + 1)
                    act.activation(vin[:, 4 * half:4 * half + 4, :].rearrange("p c s -> p (c s)"),
                                   psV[:, half, :], ACT.Copy).then_inc(v_ready, 1)

            def copy_u(q, u, halves=(0, 1)):
                for half in halves:
                    act.wait_ge(u_ready, q * 2 + half + 1)
                    if half == 0 and not isinstance(q, int):
                        act.wait_ge(y_ready, q * YQ - YQ)
                    rows = slice(4 * half, 4 * half + 4)
                    act.activation(st[u][:, rows, :, :].rearrange("p c d b -> p c (d b)"),
                                   psU[:, rows, 0:(ND - 1) * B], ACT.Copy).then_inc(u_copied, 1)

            def take_coef(q):
                if isinstance(q, int) and q == 0:
                    act.wait_ge(coef_ready, 4)
                act.activation(coef_re[:], coef[:, bass.ds(q * G, G), 0], ACT.Copy).then_inc(coef_re_ready, 1)

            def k_rows(q):
                act.wait_ge(k_made, q + 1)
                if not (isinstance(q, int) and q == 0):
                    act.wait_ge(k_stored, q * 16)
                rows = k_bank(q).rearrange("p (s j) -> p s j", s=2)
                act.activation(krow[:, :, 1:Q], rows[:, :, 1:Q], ACT.Copy).then_inc(krow_ready, 1)
                for slot in range(2):
                    act.activation(krow[:, slot, 0:1], rows[:, slot, 0:1], ACT.Identity,
                                   bias=d_sb[:, bass.ds(q, 1), slot]).then_inc(krow_ready, 1)
                take_coef(q + 1)

            def split_w(g):
                act.wait_ge(w_eye, g + 1)
                act.activation(w_hi[:, bass.ds(g, 1), :], w_raw[:, bass.ds(g, 1), :],
                               ACT.Copy).then_inc(w_hi_ready, 1)

            def take_y(g, r):
                act.wait_ge(y_ready, g * YQ + r + 1)
                y = psY[:, r % 2, :].rearrange("p (a f) -> p a f", a=2)
                if isinstance(g, int) and g in (0, NG - 1):
                    y = psU[:, 2 * r:2 * r + 2, :]
                act.activation(x[:, bass.ds(g * G + 2 * r, 2), :], y, ACT.Copy).then_inc(y_taken, 1)

            act.dma_start(cst[:], consts).then_inc(in_small, 16)
            act.dma_start(bias_in, bias2).then_inc(in_bias, 16)
            act.wait_ge(in_bias, 16)
            act.activation(b_stk[0][ones_rows, :], bias_in, ACT.Copy).then_inc(bias_step, 1)
            act.wait_ge(in_small, 64)
            act.wait_ge(bias_step, 1)
            act.activation(bias_hi, b_stk[0][ones_rows, :].bitcast(F32), ACT.Identity,
                           scale=cst[ones_rows, C_SEL:C_SEL + 1]).then_inc(bias_step, 1)
            act.activation(bias_in, bias_in, ACT.Identity,
                           scale=cst[ones_rows, C_SEL + 1:C_SEL + 2]).then_inc(bias_step, 1)
            tmp = st[1][:].rearrange("p g d b -> p (g d b)")
            act.wait_ge(rates_ready, 2)
            act.activation(tmp[:, 4 * H:5 * H], tmp[:, 2 * H:3 * H], ACT.Tanh, scale=0.5).then_inc(act_param, 1)
            act.activation(tmp[:, 5 * H:6 * H], tmp[:, 2 * H:3 * H], ACT.Exp, scale=float(Q)).then_inc(act_param, 1)
            turns(0, range(G // 2, G))
            act.wait_ge(lam_args, 1)
            act.activation(modes[:, 0:H, :], modes[:, 0:H, :], ACT.Exp).then_inc(modes_ready, 1)
            act.wait_ge(lam_args, 2)
            act.activation(tmp[:, 8 * H:12 * H], tmp[:, 8 * H:12 * H], ACT.Sin, scale=TWO_PI).then_inc(act_param, 1)
            sines(0)
            turns(1, range(0, 6))
            take_coef(0)
            turns(1, range(6, G))
            copy_e(0, 0)
            k_rows(0)
            copy_v(0)
            sines(1)
            copy_u(0, 0)
            copy_e(1, 1)
            copy_v(1)
            sines(2)
            copy_u(1, 1)

            def group(g, u):
                k_rows(g + 1)
                split_w(g)
                parts = ((0, 8, 8, 8, 8) if isinstance(g, int) and g == 0 else (0, 1, 4, 7, 8))
                for r in range(YQ):
                    if parts[r + 1] > parts[r]:
                        turns(g + 3, range(parts[r], parts[r + 1]))
                    take_y(g, r)
                copy_v(g + 2)
                copy_e(g + 2, u)
                copy_u(g + 2, u, (0,))
                if isinstance(g, int) and g == 0:
                    copy_u(g + 2, u, (1,))
                    sines(g + 3)
                else:
                    sines(g + 3)
                    copy_u(g + 2, u, (1,))

            group(0, 0)
            group(1, 1)
            with act.Fori(1, 3) as i:
                for u in range(2):
                    group(i * 2 + u, u)
            k_rows(7)
            split_w(6)
            for r in range(YQ):
                take_y(6, r)
            split_w(7)
            act.wait_ge(bias_ready, 1)
            act.activation(b_stk[1][ones_rows, :], b_stk[0][ones_rows, :].bitcast(F32), ACT.Copy).then_inc(bias_ready, 1)
            take_y(7, 0)

            def split_x(t, u):
                act.wait_ge(out_ready, t * 2 + 2)
                act.wait_ge(x1_ready, t)
                act.activation(xs_hi[u][:].rearrange("p d f -> p (d f)"),
                               xt[u][:].rearrange("p d b h -> p (d b h)"), ACT.Copy).then_inc(xs_hi_ready, 1)

            def gather_a(t, u, i):
                act.wait_ge(in_a[u], i * 32 + 32)
                act.activation(a_f[u][:].rearrange("p c (k r) -> p c k r", k=2),
                               a_raw[u][:].rearrange("p k (c r) -> p c k r", r=R), ACT.Copy).then_inc(a_ready, 1)

            def take(t, u, i):
                for half in range(2):
                    act.wait_ge(out_ready, t * 2 + 4 + half + 1)
                    if half == 0:
                        act.wait_ge(out_stored[u], i * 32 + 32)
                    act.activation(res[u][:, 512 * half:512 * half + 512],
                                   psU[:, 4 * u + 2 * half:4 * u + 2 * half + 2, :].rearrange("p a f -> p (a f)"),
                                   ACT.Copy).then_inc(out_taken, 1)

            def split_first(rows, count):
                act.wait_ge(x1_first, count)
                act.activation(xs_hi[0][:].rearrange("p d (b h) -> p d b h", b=2)[:, :, :, rows],
                               xt[0][:, :, :, rows], ACT.Copy).then_inc(first_hi, 1)

            gather_a(0, 0, 0)
            take_y(7, 1)
            split_first(slice(0, EARLY), 1)
            take_y(7, 2)
            take_y(7, 3)
            split_first(slice(EARLY, H), 2)
            with act.Fori(0, NT // 2 - 1) as i:
                for u in range(2):
                    t = i * 2 + u
                    split_x(t + 1, 1 - u)
                    gather_a(t + 1, 1 - u, i + u)
                    take(t, u, i)
            split_x(NT - 1, 1)
            gather_a(NT - 1, 1, NT // 2 - 1)
            take(NT - 2, 0, NT // 2 - 1)
            take(NT - 1, 1, NT // 2 - 1)

        @block.vector
        def _(dve):
            count = [0]

            def step(ins):
                mark(ins)
                dve.wait_ge(dve_step, count[0])

            def mark(ins):
                count[0] += 1
                ins.then_inc(dve_step, 1)

            tmp = st[1][:].rearrange("p g d b -> p (g d b)")

            def col(k, n=1):
                return tmp[:, k * H:(k + n) * H]

            def whole(q):
                dve.wait_ge(turn_ready, q + 1)
                if not (isinstance(q, int) and q == 0):
                    dve.wait_ge(pows_ready, q * 2)
                dve.tensor_scalar(phase[:], turn[:], ROUND, -ROUND, ALU.add, ALU.add).then_inc(whole_ready, 1)

            def scan(q, u, fillers, helped=False):
                base = scan_base(q)
                size = 4 if helped else 5
                fillers = list(fillers)

                def fill():
                    piece = fillers.pop(0) if fillers else None
                    if piece:
                        piece[0](*piece[1:])

                s = st[u]
                own = lam_own[:, bass.ds(q * G, G)].unsqueeze(2).to_broadcast([P, G, B])
                cross = lam_cross[:, bass.ds(q * G, G)].unsqueeze(2).to_broadcast([P, G, B])
                dve.wait_ge(u_copied, q * 2 + 2)
                if not (isinstance(q, int) and q == 0):
                    dve.wait_ge(scan_step, base)
                for d in range(1, ND - 1):
                    done = base + size * (d - 1)
                    if d > 1:
                        fill()
                        dve.wait_ge(scan_step, done)
                    dve.tensor_tensor(sa[:], s[:, :, d - 1, :], own, ALU.mult).then_inc(scan_step, 1)
                    dve.tensor_tensor(sx[0:N], s[N:P, :, d - 1, :], cross[N:P], ALU.mult).then_inc(scan_step, 1)
                    if not helped:
                        dve.tensor_tensor(sx[N:P], s[0:N, :, d - 1, :], cross[0:N], ALU.mult).then_inc(scan_step, 1)
                    dve.wait_ge(scan_step, done + 1)
                    dve.tensor_tensor(s[:, :, d, :], s[:, :, d, :], sa[:], ALU.add).then_inc(scan_step, 1)
                    fill()
                    dve.wait_ge(scan_step, done + size - 1)
                    if helped:
                        dve.wait_ge(crossed, (HELPED if q else 0) + d)
                    dve.tensor_tensor(s[:, :, d, :], s[:, :, d, :], sx[:], ALU.add).then_inc(scan_step, 1)
                while fillers:
                    fill()

            dt, ea, decay, theta, tanh, eq = (col(k) for k in range(6))
            are, args = col(6), col(8, 4)
            cr, ci, aim = prm[:, 3, :], prm[:, 4, :], prm[:, 2, :]
            dve.memset(zero, 0.0).then_inc(zeros_made, 1)
            for u in range(2):
                dve.memset(h_stk[u][ones_rows, :].bitcast(F32), 1.0).then_inc(ones_made, 1)
            dve.memset(mag[:, :, 0:1], 1.0).then_inc(mag_ready, 1)
            mark(dve.memset(modes[:, H:H + G, :], 0.0))
            mark(dve.memset(coef[:, H:H + G, :], 0.0))
            step(dve.memset(freq[:, H:H + G], 0.0))
            logs = prm[:, 0:2, :].rearrange("p k h -> p (k h)")
            k2, r2, q2_, p2 = col(12, 2), col(14, 2), col(16, 2), col(18, 2)
            dve.wait_ge(in_par, 16)
            step(dve.tensor_scalar(k2, logs, LOG2E, ROUND, ALU.mult, ALU.add))
            step(dve.tensor_scalar(k2, k2, -ROUND, -126.0, ALU.add, ALU.max))
            step(dve.scalar_tensor_tensor(r2, k2, -LN2_HI, logs, ALU.mult, ALU.add))
            step(dve.scalar_tensor_tensor(r2, k2, -LN2_LO, r2, ALU.mult, ALU.add))
            mark(dve.tensor_scalar(p2.bitcast(I32), k2, 127.0, 8388608.0, ALU.add, ALU.mult))
            step(dve.tensor_scalar(q2_, r2, 1.0 / 5040, 1.0 / 720, ALU.mult, ALU.add))
            step(dve.tensor_tensor(q2_, q2_, r2, ALU.mult))
            for c in (1.0 / 120, 1.0 / 24, 1.0 / 6, 0.5, 1.0):
                step(dve.scalar_tensor_tensor(q2_, q2_, c, r2, ALU.add, ALU.mult))
            step(dve.scalar_tensor_tensor(col(0, 2), q2_, 1.0, p2, ALU.add, ALU.mult))
            dve.tensor_tensor(theta, aim, dt, ALU.mult).then_inc(rates_ready, 1)
            dve.scalar_tensor_tensor(decay, ea, -1.0, dt, ALU.mult, ALU.mult).then_inc(rates_ready, 1)
            dve.wait_ge(rates_ready, 2)
            dve.tensor_scalar(freq[:, 0:H], theta, 1.0 / (2 * PI), None, ALU.mult).then_inc(freq_ready, 1)
            dve.tensor_scalar(are, ea, -1.0, None, ALU.mult).then_inc(freq_ready, 1)
            dve.wait_ge(in_small, 64)
            jm = cst[:, C_EXP:C_EXP + MA + MB].unsqueeze(1).to_broadcast([P, H, MA + MB])
            dve.tensor_tensor(modes[:, 0:H, :], decay.unsqueeze(2).to_broadcast([P, H, MA + MB]), jm,
                              ALU.mult).then_inc(lam_args, 1)
            dve.wait_ge(freq_ready, 2)
            f = freq[:, 0:H]
            mark(dve.tensor_scalar(args[:, 0:H], f, float(Q), 0.25, ALU.mult, ALU.add))
            mark(dve.tensor_scalar(args[:, H:2 * H], f, float(Q), cst[:, C_OFFX:C_OFFX + 1], ALU.mult, ALU.add))
            step(dve.tensor_copy(args[:, 2 * H:3 * H], f))
            wh = col(12, 3)
            step(dve.tensor_scalar(wh, args[:, 0:3 * H], ROUND, -ROUND, ALU.add, ALU.add))
            step(dve.tensor_tensor(args[:, 0:3 * H], args[:, 0:3 * H], wh, ALU.subtract))
            dve.tensor_scalar(args[:, 3 * H:4 * H], args[:, 2 * H:3 * H], 0.5, None, ALU.mult).then_inc(lam_args, 1)
            om, em1 = col(15), col(16)
            dve.wait_ge(act_param, 1)
            step(dve.tensor_scalar(om, tanh, -1.0, 1.0, ALU.mult, ALU.add))
            step(dve.reciprocal(om, om))
            step(dve.scalar_tensor_tensor(em1, tanh, 2.0, om, ALU.mult, ALU.mult))
            dve.wait_ge(turn_half, 1)
            whole(0)
            fraction(dve, 0)
            den, wr, wi = col(22), col(24), col(26)
            dve.wait_ge(two_c, 3)
            step(dve.reciprocal(den, den))
            mark(dve.scalar_tensor_tensor(wr, wr, 2.0, den, ALU.mult, ALU.mult))
            mark(dve.scalar_tensor_tensor(wi, wi, 2.0, den, ALU.mult, ALU.mult))
            s_own, s_cross, s_th, s_half = (args[:, k * H:(k + 1) * H] for k in range(4))
            sq, cosm, nr, ni, m1, m2, m3, m4 = (col(k) for k in (20, 21, 12, 13, 14, 15, 17, 18))
            dve.wait_ge(act_param, 3)
            mark(dve.tensor_tensor(sq, s_half, s_half, ALU.mult))
            step(dve.scalar_tensor_tensor(ni, em1, 1.0, s_th, ALU.add, ALU.mult))
            step(dve.tensor_scalar(cosm, sq, -2.0, 1.0, ALU.mult, ALU.add))
            step(dve.tensor_tensor(cosm, em1, cosm, ALU.mult))
            step(dve.scalar_tensor_tensor(nr, sq, -2.0, cosm, ALU.mult, ALU.add))
            mark(dve.tensor_tensor(m1, nr, wr, ALU.mult))
            mark(dve.tensor_tensor(m2, ni, wi, ALU.mult))
            mark(dve.tensor_tensor(m3, nr, wi, ALU.mult))
            step(dve.tensor_tensor(m4, ni, wr, ALU.mult))
            dve.tensor_tensor(coef[0:N, 0:H, 0], m1[0:N, :], m2[0:N, :], ALU.subtract).then_inc(coef_ready, 1)
            dve.tensor_tensor(coef[0:N, 0:H, 1], m3[0:N, :], m4[0:N, :], ALU.add).then_inc(coef_ready, 1)
            dve.tensor_tensor(coef[N:P, 0:H, 0], m3[N:P, :], m4[N:P, :], ALU.add).then_inc(coef_ready, 1)
            dve.tensor_tensor(coef[N:P, 0:H, 1], m2[N:P, :], m1[N:P, :], ALU.subtract).then_inc(coef_ready, 1)
            rotation(dve, 0)
            whole(1)
            fraction(dve, 1)
            dve.tensor_tensor(lam_own[:], s_own, eq, ALU.mult).then_inc(lam_ready, 1)
            dve.tensor_tensor(lam_cross[:], s_cross, eq, ALU.mult).then_inc(lam_ready, 1)
            dve.tensor_tensor(mask[:], cst[:, C_LPOS:C_LPOS + ND].unsqueeze(2).to_broadcast([P, ND, B]),
                              len_sb[:].unsqueeze(1).to_broadcast([P, ND, B]), ALU.is_lt).then_inc(mask_ready, 1)
            rotation(dve, 1)
            powers(dve, 1, 0)
            powers(dve, 1, 1)
            whole(2)
            fraction(dve, 2)
            dve.wait_ge(lam_ready, 2)
            scan(0, 0, [], helped=True)

            def group(g, u):
                scan(g + 1, 1 - u, [None] * 6 + [(whole, g + 3)])

            for u in range(2):
                group(u, u)
            with dve.Fori(1, 3) as i:
                for u in range(2):
                    group(i * 2 + u, u)
            scan(7, 1, [], helped=True)

            def x1_early(rows, n, taken):
                dve.wait_ge(y_taken, taken)
                z = x[:].rearrange("p h (d b) -> p d b h", b=B)[:, :, 0:2, rows]
                m = mask[:, :, 0:2].unsqueeze(3).to_broadcast([P, ND, 2, rows.stop - rows.start])
                dve.tensor_tensor(zt[:, :, :, rows], z, m, ALU.mult).then_inc(first_masked, 1)
                dve.wait_ge(in_xt[0], 16)
                dve.wait_ge(first_masked, n)
                dve.tensor_tensor(xt[0][:, :, :, rows], xt[0][:, :, :, rows], zt[:, :, :, rows],
                                  ALU.add).then_inc(x1_first, 1)

            def low_early(rows, n, last=False):
                dve.wait_ge(first_hi, n)
                ins = dve.tensor_tensor(xs_lo[0][:].rearrange("p d (b h) -> p d b h", b=2)[:, :, :, rows],
                                        xt[0][:, :, :, rows],
                                        xs_hi[0][:].bitcast(F32).rearrange("p d (b h) -> p d b h", b=2)[:, :, :, rows],
                                        ALU.subtract)
                if last:
                    ins.then_inc(xs_lo_ready, 1)

            def make_x1(t, u, i):
                z = x[:].rearrange("p h (d b) -> p d b h", b=B)[:, :, bass.ds(t * 2, 2), :]
                m = mask[:, :, bass.ds(t * 2, 2)].unsqueeze(3).to_broadcast([P, ND, 2, H])
                dve.tensor_tensor(zt[:], z, m, ALU.mult).then_inc(z_masked, 1)
                dve.wait_ge(in_xt[u], i * 16 + 16)
                dve.wait_ge(z_masked, t)
                dve.tensor_tensor(xt[u][:].rearrange("p d b h -> p (d b h)"),
                                  xt[u][:].rearrange("p d b h -> p (d b h)"),
                                  zt[:].rearrange("p d b h -> p (d b h)"), ALU.add).then_inc(x1_ready, 1)

            def low_x(t, u):
                dve.wait_ge(xs_hi_ready, t)
                dve.tensor_tensor(xs_lo[u][:].rearrange("p d f -> p (d f)"),
                                  xt[u][:].rearrange("p d b h -> p (d b h)"),
                                  xs_hi[u][:].rearrange("p d f -> p (d f)").bitcast(F32),
                                  ALU.subtract).then_inc(xs_lo_ready, 1)

            def stack_b(t, u, i):
                dve.wait_ge(in_b[u], i * 32 + 32)
                dve.wait_ge(out_ready, t * 2 + 2)
                dve.tensor_copy(b_stk[u][0:32, :], b_raw[u][:]).then_inc(b_hi_ready, 1)
                dve.tensor_copy(b_stk[u][32:64, :], b_raw[u][:]).then_inc(b_hi_ready, 1)
                dve.wait_ge(b_hi_ready, t * 2 + 2)
                dve.tensor_tensor(b_stk[u][64:96, :], b_raw[u][:], b_stk[u][0:32, :].bitcast(F32),
                                  ALU.subtract).then_inc(b_ready, 1)

            def stack_h(t, u):
                dve.wait_ge(h_ready, t + 1)
                own = cst[0:2 * R, C_BM:C_BM + P]
                h = h_sum[:]
                dve.tensor_copy(h, psY[0:32, u, 0:P]).then_inc(h_step, 1)
                for k in range(1, CG):
                    dve.wait_ge(h_step, t * HS + k)
                    dve.tensor_tensor(h, psY[32 * k:32 * k + 32, u, 0:P], h, ALU.add).then_inc(h_step, 1)
                dve.wait_ge(h_step, t * HS + CG)
                dve.tensor_tensor(h_f32[:], h, own, ALU.mult).then_inc(h_step, 1)
                dve.tensor_tensor(h_stk[u][0:32, :], h, own, ALU.mult).then_inc(h_step, 1)
                dve.tensor_tensor(h_stk[u][64:96, :], h, own, ALU.mult).then_inc(h_step, 1)
                dve.wait_ge(h_step, t * HS + CG + 3)
                dve.tensor_tensor(h_stk[u][32:64, :], h_f32[:], h_stk[u][0:32, :].bitcast(F32),
                                  ALU.subtract).then_inc(h_step, 1)

            dve.wait_ge(mask_ready, 1)
            x1_early(slice(0, EARLY), 1, 2 + (NG - 1) * YQ)
            low_early(slice(0, EARLY), 1)
            x1_early(slice(EARLY, H), 2, 2 + NG * YQ)
            low_early(slice(EARLY, H), 2, last=True)
            stack_b(0, 0, 0)
            stack_h(0, 0)
            make_x1(1, 1, 0)
            with dve.Fori(0, NT // 2 - 1) as i:
                for u in range(2):
                    t = i * 2 + u
                    low_x(t + 1, 1 - u)
                    stack_b(t + 1, 1 - u, i + u)
                    make_x1(t + 2, u, i + 1)
                    stack_h(t + 1, 1 - u)
            low_x(NT - 1, 1)
            stack_b(NT - 1, 1, NT // 2 - 1)
            stack_h(NT - 1, 1)

        @block.gpsimd
        def _(pool):
            def magnitude(q):
                if not (isinstance(q, int) and q == 0):
                    pool.wait_ge(pows_ready, q * 2)
                else:
                    pool.wait_ge(modes_ready, 1)
                t = modes[:, bass.ds(q * G, G), :]
                pool.tensor_tensor(mag[:, :, 1:NJ].rearrange("p c (m n) -> p c m n", m=MA),
                                   t[:, :, MB:MB + MA].unsqueeze(3).to_broadcast([P, G, MA, MB]),
                                   t[:, :, 0:MB].unsqueeze(2).to_broadcast([P, G, MA, MB]),
                                   ALU.mult).then_inc(mag_ready, 1)

            def eye_w(g):
                pool.wait_ge(in_w, g * 16 + 16)
                d = w_raw[:, bass.ds(g, 1), bass.ds(g * Q, Q)]
                pool.tensor_tensor(d, d, cst[:, C_EYE:C_EYE + P].unsqueeze(1), ALU.add).then_inc(w_eye, 1)

            def low_w(g):
                pool.wait_ge(w_hi_ready, g + 1)
                pool.tensor_tensor(w_lo[:, bass.ds(g, 1), :], w_raw[:, bass.ds(g, 1), :], w_hi[:, bass.ds(g, 1), :].bitcast(F32),
                                   ALU.subtract).then_inc(w_lo_ready, 1)

            pool.memset(credit[0:1, 0:1], 0.0).then_inc(y_taken, 2)
            pool.memset(credit[0:1, 1:2], 0.0).then_inc(out_ready, 4)
            pool.memset(credit[0:1, 2:3], 0.0).then_inc(out_taken, 4)
            pool.memset(credit[0:1, 3:4], 0.0).then_inc(out_stored[0], 32)
            pool.memset(credit[0:1, 4:5], 0.0).then_inc(out_stored[1], 32)
            tmp = st[1][:].rearrange("p g d b -> p (g d b)")

            def first_turns(q, part, done):
                for c in part:
                    ins = pool.tensor_scalar(turn[:, c, :], cst[:, C_J:C_J + NJ], freq[:, q * G + c:q * G + c + 1],
                                             cst[:, C_OFF:C_OFF + 1], ALU.mult, ALU.add)
                ins.then_inc(done, 1)

            def help_scan(q, u):
                pool.wait_ge(lam_ready, 2)
                pool.wait_ge(u_copied, q * 2 + 2)
                cross = lam_cross[0:N, q * G:q * G + G].unsqueeze(2).to_broadcast([N, G, B])
                for d in range(1, ND - 1):
                    if scan_base(q) + 4 * (d - 1) > 0:
                        pool.wait_ge(scan_step, scan_base(q) + 4 * (d - 1))
                    pool.tensor_tensor(sx[N:P], st[u][0:N, :, d - 1, :], cross, ALU.mult).then_inc(crossed, 1)

            pool.wait_ge(in_small, 64)
            pool.wait_ge(freq_ready, 2)
            first_turns(0, range(G // 2), turn_half)

            def col(k):
                return tmp[:, k * H:(k + 1) * H]
            are, aim, cr, ci = col(6), prm[:, 2, :], prm[:, 3, :], prm[:, 4, :]
            for o, a, b in ((22, are, are), (23, aim, aim), (24, cr, are), (25, ci, aim),
                            (26, ci, are), (27, cr, aim)):
                pool.tensor_tensor(col(o), a, b, ALU.mult).then_inc(pool_step, 1)
            pool.wait_ge(pool_step, 6)
            pool.tensor_tensor(col(22), col(22), col(23), ALU.add).then_inc(two_c, 1)
            pool.tensor_tensor(col(24), col(24), col(25), ALU.add).then_inc(two_c, 1)
            pool.tensor_tensor(col(26), col(26), col(27), ALU.subtract).then_inc(two_c, 1)
            magnitude(0)
            powers(pool, 0, 0)
            powers(pool, 0, 1)
            magnitude(1)
            pool.wait_ge(frac_ready, 2)
            first_turns(2, range(G), turn_ready)
            magnitude(2)
            eye_w(0)
            pool.wait_ge(w_eye, 1)
            help_scan(0, 0)
            pool.wait_ge(crossed, HELPED)
            rotation(pool, 2)
            def group(g):
                powers(pool, g + 2, 0)
                powers(pool, g + 2, 1)
                magnitude(g + 3)
                low_w(g)
                fraction(pool, g + 3)
                eye_w(g + 1)
                rotation(pool, g + 3)
                if isinstance(g, int) and g == 0:
                    pool.wait_ge(bias_step, 3)
                    pool.wait_ge(rot_ready, 4)
                    pool.tensor_tensor(b_stk[0][ones_rows, :], bias_hi, bias_in, ALU.add).then_inc(bias_ready, 1)
                    pool.wait_ge(bias_ready, 1)

            for g in range(2):
                group(g)
            with pool.Fori(1, 3) as i:
                for u in range(2):
                    group(i * 2 + u)
            eye_w(7)
            pool.wait_ge(w_eye, NG)
            help_scan(7, 1)
            pool.wait_ge(crossed, 2 * HELPED)
            low_w(6)
            low_w(7)


def kernel(**inputs):
    import numpy as np
    import concourse.bacc as bacc
    from concourse.bass_utils import run_bass_kernel_spmd

    a = {k: np.asarray(v) for k, v in inputs.items()}
    both = lambda m: np.concatenate([m, m], axis=0)
    ld = np.broadcast_to(a["L0_cond_log_dt"][None, :], (P, H))
    c = a["L0_cond_C"]
    arrays = {
        "xT": np.ascontiguousarray(a["x"].reshape(B, H, ND, Q)[..., ::-1].transpose(3, 1, 2, 0)
                                   .reshape(Q, H, ND * B)),
        "xB": np.ascontiguousarray(a["x"].reshape(NT, 2, H, ND, Q).transpose(0, 4, 3, 1, 2)
                                   .reshape(NT * Q, ND * 2 * H)),
        "par": np.ascontiguousarray(np.stack(
            [ld, both(a["L0_cond_log_A_real"].T), both(a["L0_cond_A_imag"].T),
             both(c[:, :, 0].T), both(c[:, :, 1].T)], axis=1)),
        "dvec": np.ascontiguousarray(np.repeat(a["L0_cond_D"].reshape(NG, 2, 4).transpose(2, 0, 1), 32, axis=0)),
        "lens": np.ascontiguousarray(np.broadcast_to(a["itok_B_78_3631"][None, :], (P, B))),
        "slots": np.ascontiguousarray(a["itok_B_0_23"][None, :]),
        "wT": np.ascontiguousarray(a["L1_cond_W"].T.reshape(ND, Q, L).transpose(1, 0, 2)),
        "bias2": np.ascontiguousarray(np.broadcast_to(a["L1_cond_b"][None, :], (2, L))),
        "loraA": np.ascontiguousarray(a["L1_cond_lora_As"].reshape(SLOTS, ND, Q, R).transpose(0, 2, 1, 3)
                                      .reshape(SLOTS, Q, ND * R)),
        "loraB": np.ascontiguousarray(a["L1_cond_lora_Bs"]),
        "consts": constants(),
    }
    nc = bacc.Bacc("TRN2", target_bir_lowering=False, num_devices=1)
    args = [nc.dram_tensor(n, v.shape, mybir.dt.from_np(v.dtype), kind="ExternalInput").ap()
            for n, v in arrays.items()]
    out = nc.dram_tensor("out", (B * H, L), F32, kind="ExternalOutput").ap()
    conv_then_lora(nc, *args, out)
    r = run_bass_kernel_spmd(nc, [arrays], core_ids=[0])
    return r.results[0]["out"].reshape(B, H, L)
```
